# Optimizing a Trainium2 kernel written in Bass

```python
import numpy as np
import jax
import jax.numpy as jnp

def _softmax(x, axis=-1):
    return jax.nn.softmax(x, axis=axis)

def _gelu(x):
    return jax.nn.gelu(x, approximate=True)

def _silu(x):
    return jax.nn.silu(x)

def _sigmoid(x):
    return jax.nn.sigmoid(x)

def _layernorm(x, axis=-1, eps=1e-05):
    m = jnp.mean(x, axis=axis, keepdims=True)
    v = jnp.var(x, axis=axis, keepdims=True)
    return (x - m) / jnp.sqrt(v + eps)

def _scatter_add(tgt, idx, src, axis=0):
    return tgt.at[idx].add(src)

def _segment_sum(src, seg, n):
    return jax.ops.segment_sum(src, seg, n)
kernel_name = 'mk_perceiver_d1_seqx_r8_7a944b'

def setup_inputs(seed: int=0):
    np.random.seed(seed)
    _w = jnp.asarray

    def _rec_inputs():
        import jax
        import jax.numpy as jnp
        _rk = jax.random.key(seed)
        x = 0.002226 + 0.9996 * jax.random.normal(jax.random.fold_in(_rk, 1), (4, 128, 128), jnp.float32)
        _lenS = 128 - jax.random.randint(jax.random.fold_in(_rk, 7), (4,), 0, max(1, 128 // 4) + 1, jnp.int32)
        _lenS2 = 2048 - jax.random.randint(jax.random.fold_in(_rk, 8), (4,), 0, max(1, 2048 // 4) + 1, jnp.int32)
        _ctx_1024P = jax.random.normal(jax.random.fold_in(_rk, 11), (4, 16, 128), jnp.float32)
        _ctx_1024c = jax.random.dirichlet(jax.random.fold_in(_rk, 511), 0.3 * jnp.ones((16,), jnp.float32), (4, 2048))
        _ctx_1024t = jnp.einsum('bsk,bkd->bsd', _ctx_1024c, _ctx_1024P)
        _ctx_1024t = _ctx_1024t * jax.lax.rsqrt(jnp.mean(jnp.square(_ctx_1024t)) + 1e-12) * 0.953939
        ctx_1024 = -0.000125008 + 0.999885 * (_ctx_1024t + 0.3 * jax.random.normal(jax.random.fold_in(_rk, 611), (4, 2048, 128), jnp.float32))
        _validS = jnp.arange(128)[None, :] < _lenS[:, None]
        _validS2 = jnp.arange(2048)[None, :] < _lenS2[:, None]
        _causal = jnp.tril(jnp.ones((128, 128), dtype=bool))
        mask_BxS2_bk0 = jnp.logical_not(jnp.broadcast_to(_validS2[:, :], (4, 2048)))
        return (x, ctx_1024, mask_BxS2_bk0)
    x, ctx_1024, mask_BxS2_bk0 = _rec_inputs()

    def _L0_xattn_setup():
        import jax, jax.numpy as jnp
        import numpy as np
        EPS = 1e-05

        def layer_norm(x, g, b):
            mu = jnp.mean(x, axis=-1, keepdims=True)
            var = jnp.mean((x - mu) ** 2, axis=-1, keepdims=True)
            return (x - mu) * jax.lax.rsqrt(var + EPS) * g + b
        key = jax.random.key(seed)
        ks = jax.random.split(key, 8)
        b, n, l, D = (8, 512, 64, 128)
        heads, dim_head = (16, 64)
        inner = heads * dim_head
        x = jax.random.normal(ks[0], (b, n, D), dtype=jnp.float32)
        latents = jax.random.normal(ks[1], (b, l, D), dtype=jnp.float32)
        mask = jax.random.randint(ks[2], (b, n), 0, 2) > 0
        Wq = jax.random.normal(ks[3], (D, inner), dtype=jnp.float32) * D ** (-0.5)
        Wkv = jax.random.normal(ks[4], (D, 2 * inner), dtype=jnp.float32) * D ** (-0.5)
        Wout = jax.random.normal(ks[5], (inner, D), dtype=jnp.float32) * inner ** (-0.5)
        g1 = jnp.ones((D,), jnp.float32)
        b1 = jnp.zeros((D,), jnp.float32)
        g2 = jnp.ones((D,), jnp.float32)
        b2 = jnp.zeros((D,), jnp.float32)
        return {'x': x, 'latents': latents, 'mask': mask, 'g1': g1, 'b1': b1, 'g2': g2, 'b2': b2, 'Wq': Wq, 'Wkv': Wkv, 'Wout': Wout}
    _L0_xattn_all = _L0_xattn_setup()
    _L0_xattn_in = {k: v for k, v in _L0_xattn_all.items() if k in ('g1', 'b1', 'g2', 'b2', 'Wq', 'Wkv', 'Wout')}
    del _L0_xattn_all

    def _L0_attn_setup():
        import jax, jax.numpy as jnp
        import numpy as np
        D_MODEL = 128
        N_HEADS = 16
        D_K = D_MODEL // N_HEADS
        WINDOW = 32
        BATCH = 1
        SEQ = 512
        key = jax.random.key(seed)
        ks = jax.random.split(key, 9)
        w_scale = 1.0 / np.sqrt(D_MODEL).astype(np.float32)
        return {'x': jax.random.normal(ks[0], (BATCH, SEQ, D_MODEL), jnp.float32), 'Wq': jax.random.normal(ks[1], (D_MODEL, D_MODEL), jnp.float32) * w_scale, 'bq': jnp.zeros((D_MODEL,), jnp.float32), 'Wk': jax.random.normal(ks[2], (D_MODEL, D_MODEL), jnp.float32) * w_scale, 'bk': jnp.zeros((D_MODEL,), jnp.float32), 'Wv': jax.random.normal(ks[3], (D_MODEL, D_MODEL), jnp.float32) * w_scale, 'bv': jnp.zeros((D_MODEL,), jnp.float32), 'Wo': jax.random.normal(ks[4], (D_MODEL, D_MODEL), jnp.float32) * w_scale, 'bo': jnp.zeros((D_MODEL,), jnp.float32)}
    _L0_attn_all = _L0_attn_setup()
    _L0_attn_in = {k: v for k, v in _L0_attn_all.items() if k in ('Wq', 'bq', 'Wk', 'bk', 'Wv', 'bv', 'Wo', 'bo')}
    del _L0_attn_all

    def _L0_ffn_setup():
        import jax, jax.numpy as jnp
        import numpy as np
        S, B, H = (256, 1, 128)
        E, K, F = (8, 2, 176)
        key = jax.random.key(seed)
        k1, k2, k3, k4 = jax.random.split(key, 4)
        return {'hidden_states': jax.random.normal(k1, (S, B, H), jnp.float32), 'router_weight': jax.random.normal(k2, (H, E), jnp.float32) * 0.02, 'w1': jax.random.normal(k3, (E, H, 2 * F), jnp.float32) * 0.02, 'w2': jax.random.normal(k4, (E, F, H), jnp.float32) * 0.02}
    _L0_ffn_all = _L0_ffn_setup()
    _L0_ffn_in = {k: v for k, v in _L0_ffn_all.items() if k in ('router_weight', 'w1', 'w2')}
    del _L0_ffn_all
    return {'x': x, 'ctx_1024': ctx_1024, 'mask_BxS2_bk0': mask_BxS2_bk0, 'L0_xattn_g1': _L0_xattn_in['g1'], 'L0_xattn_b1': _L0_xattn_in['b1'], 'L0_xattn_g2': _L0_xattn_in['g2'], 'L0_xattn_b2': _L0_xattn_in['b2'], 'L0_xattn_Wq': _L0_xattn_in['Wq'], 'L0_xattn_Wkv': _L0_xattn_in['Wkv'], 'L0_xattn_Wout': _L0_xattn_in['Wout'], 'L0_attn_Wq': _L0_attn_in['Wq'], 'L0_attn_bq': _L0_attn_in['bq'], 'L0_attn_Wk': _L0_attn_in['Wk'], 'L0_attn_bk': _L0_attn_in['bk'], 'L0_attn_Wv': _L0_attn_in['Wv'], 'L0_attn_bv': _L0_attn_in['bv'], 'L0_attn_Wo': _L0_attn_in['Wo'], 'L0_attn_bo': _L0_attn_in['bo'], 'L0_ffn_router_weight': _L0_ffn_in['router_weight'], 'L0_ffn_w1': _L0_ffn_in['w1'], 'L0_ffn_w2': _L0_ffn_in['w2']}

def reference(x, ctx_1024, mask_BxS2_bk0, L0_xattn_g1, L0_xattn_b1, L0_xattn_g2, L0_xattn_b2, L0_xattn_Wq, L0_xattn_Wkv, L0_xattn_Wout, L0_attn_Wq, L0_attn_bq, L0_attn_Wk, L0_attn_bk, L0_attn_Wv, L0_attn_bv, L0_attn_Wo, L0_attn_bo, L0_ffn_router_weight, L0_ffn_w1, L0_ffn_w2):
    import jax
    import jax.numpy as jnp

    def _L0_xattn_ref(x, latents, mask, g1, b1, g2, b2, Wq, Wkv, Wout):
        import jax, jax.numpy as jnp
        import numpy as np
        EPS = 1e-05

        def layer_norm(x, g, b):
            mu = jnp.mean(x, axis=-1, keepdims=True)
            var = jnp.mean((x - mu) ** 2, axis=-1, keepdims=True)
            return (x - mu) * jax.lax.rsqrt(var + EPS) * g + b
        heads, dim_head = (16, 64)
        b, n, D = x.shape
        l = latents.shape[1]
        xn = layer_norm(x, g1, b1)
        ln_lat = layer_norm(latents, g2, b2)
        q = ln_lat @ Wq
        kv = jnp.concatenate([xn, ln_lat], axis=1) @ Wkv
        k, v = jnp.split(kv, 2, axis=-1)

        def to_heads(t):
            return t.reshape(t.shape[0], t.shape[1], heads, dim_head).transpose(0, 2, 1, 3)
        q, k, v = (to_heads(q), to_heads(k), to_heads(v))
        scale = 1.0 / np.sqrt(np.sqrt(dim_head)).astype(np.float32)
        weight = jnp.einsum('bhld,bhnd->bhln', q * scale, k * scale)
        full_mask = jnp.concatenate([mask, jnp.ones((b, l), dtype=bool)], axis=1)
        neg = -jnp.finfo(weight.dtype).max
        weight = jnp.where(full_mask[:, None, None, :], weight, neg)
        weight = jax.nn.softmax(weight.astype(jnp.float32), axis=-1).astype(q.dtype)
        out = jnp.einsum('bhln,bhnd->bhld', weight, v)
        out = out.transpose(0, 2, 1, 3).reshape(b, l, heads * dim_head)
        return out @ Wout

    def _L0_attn_ref(x, Wq, bq, Wk, bk, Wv, bv, Wo, bo):
        import jax, jax.numpy as jnp
        import numpy as np
        D_MODEL = 128
        N_HEADS = 16
        D_K = D_MODEL // N_HEADS
        WINDOW = 32
        BATCH = 1
        SEQ = 512
        B, S, D = x.shape
        H, dk = (N_HEADS, D_K)

        def proj(W, b):
            return (x @ W + b).reshape(B, S, H, dk).transpose(0, 2, 1, 3)
        q = proj(Wq, bq)
        k = proj(Wk, bk)
        v = proj(Wv, bv)
        scores = jnp.einsum('bhqd,bhkd->bhqk', q, k) / np.sqrt(dk).astype(np.float32)
        idx = jnp.arange(S)
        local = jnp.abs(idx[:, None] - idx[None, :]) <= WINDOW // 2
        scores = jnp.where(local[None, None], scores, jnp.float32(-1000000000.0))
        attn = jax.nn.softmax(scores, axis=-1)
        out = jnp.einsum('bhqk,bhkd->bhqd', attn, v)
        out = out.transpose(0, 2, 1, 3).reshape(B, S, D)
        return out @ Wo + bo

    def _L0_ffn_ref(hidden_states, router_weight, w1, w2):
        import jax, jax.numpy as jnp
        import numpy as np
        S, B, H = (256, 1, 128)
        E, K, F = (8, 2, 176)
        s, b, h = hidden_states.shape
        x = hidden_states.reshape(-1, h)
        logits = x @ router_weight
        probs = jax.nn.softmax(logits, axis=-1)
        _, topk_idx = jax.lax.top_k(probs, K)
        routing_map = jax.nn.one_hot(topk_idx, E, dtype=probs.dtype).sum(axis=1)
        local_probs = probs * routing_map
        y = jnp.einsum('th,ehf->tef', x, w1)
        y1, y2 = jnp.split(y, 2, axis=-1)
        g = jax.nn.silu(y1) * y2
        o = jnp.einsum('tef,efh->teh', g, w2)
        out = jnp.einsum('teh,te->th', o, local_probs)
        return out.reshape(s, b, h)
    x = x + _L0_xattn_ref(ctx_1024, _layernorm(x, axis=-1), mask_BxS2_bk0, L0_xattn_g1, L0_xattn_b1, L0_xattn_g2, L0_xattn_b2, L0_xattn_Wq, L0_xattn_Wkv, L0_xattn_Wout)
    x = x + _L0_attn_ref(_layernorm(x, axis=-1), L0_attn_Wq, L0_attn_bq, L0_attn_Wk, L0_attn_bk, L0_attn_Wv, L0_attn_bv, L0_attn_Wo, L0_attn_bo)
    x = x + _L0_ffn_ref(_layernorm(x, axis=-1), L0_ffn_router_weight, L0_ffn_w1, L0_ffn_w2)
    return x

_drawn_inputs = setup_inputs


def setup_inputs(seed=0):
    import zlib

    import numpy as np

    out = dict(_drawn_inputs(seed))
    spreads = {'L0_xattn_g1': (1.0, 0.2),
     'L0_xattn_b1': (0.0, 0.1),
     'L0_xattn_g2': (1.0, 0.2),
     'L0_xattn_b2': (0.0, 0.1),
     'L0_attn_bq': (0.0, 0.417),
     'L0_attn_bk': (0.0, 0.8),
     'L0_attn_bv': (0.0, 0.1),
     'L0_attn_bo': (0.0, 0.1)}
    factors = {'L0_ffn_router_weight': 8.0, 'L0_ffn_w1': 8.0, 'L0_ffn_w2': 8.0}
    for name, (base, spread) in spreads.items():
        noise = np.random.default_rng([zlib.crc32(name.encode()), seed]).standard_normal(out[name].shape)
        drawn = base * np.exp(spread * noise) if base else spread * noise
        out[name] = jnp.asarray(drawn.astype(out[name].dtype))
    for name, factor in factors.items():
        out[name] = (out[name] * factor).astype(out[name].dtype)
    return out
```

```python
from contextlib import ExitStack

import concourse.bass as bass
from concourse import mybir

ALU = mybir.AluOpType
ACT = mybir.ActivationFunctionType
AX_X = mybir.AxisListType.X
F32 = mybir.dt.float32
F16 = mybir.dt.float16
BF16 = mybir.dt.bfloat16
I32 = mybir.dt.int32
U8 = mybir.dt.uint8

EPS = 1e-5
MASKED = -1e30
OUTSIDE = -3e9
WINDOW = 32


def perceiver_block(nc, x, ctxt, mask, g1, b1, g2, b2, Wq, Wkv, Wout,
                    aWq, abq, aWk, abk, aWv, abv, aWo, abo, rw, w1, w2, out):
    B, L, D = x.shape
    S = ctxt.shape[1]
    INNER = Wq.shape[1]
    DH = 64
    H = INNER // DH
    NC = S // 128
    NJ = INNER // 128
    HG = H // 2
    GC = HG * L
    QB = H * L
    E, _, F2 = w1.shape
    F = F2 // 2
    FH = F // 2
    AH = 16
    DK = D // AH
    ASCALE = DK ** -0.5
    XSCALE = 1.0 / 8.0
    SHIFT = 4.0
    TSCALE = 2.0 ** -5
    BL = B * L

    with ExitStack() as ctx:
        def sb(name, shape, dt):
            return ctx.enter_context(nc.sbuf_tensor(name, shape, dt))

        def sem(name):
            return ctx.enter_context(nc.semaphore(name))

        ps = ctx.enter_context(nc.psum_tensor("ps", [128, 8, 512], F32))

        ident = sb("ident", [128, 128], F32)
        identh = sb("identh", [128, 128], F16)
        identb = sb("identb", [128, 128], BF16)
        fold = sb("fold", [128, 128], F32)
        gt = sb("gt", [128, 2, 128], F32)
        gb = sb("gb", [128, 4], F32)
        zero2 = sb("zero2", [128, 130], F16)
        neghalf = sb("neghalf", [128, 64], F32)
        weight = sb("weight", [1, 64], F32)
        band = sb("band", [128, 128], BF16)
        headmask = sb("headmask", [128, 4], F32)
        tri = sb("tri", [128, 8, 8], F32)
        mk = sb("mk", [B * NC, 128], U8)
        mkf = sb("mkf", [B * NC, 128], F32)
        flag = sb("flag", [B * NC, 1], F32)
        lastc = sb("lastc", [1, 64], F32)
        metaf = sb("metaf", [1, 12], F32)
        meta = sb("meta", [1, 12], I32)
        mbias = sb("mbias", [128, B * NC], F32)
        xs = sb("xs", [128, B, D], F32)
        xn = sb("xn", [128, B, D], F32)
        st = sb("st", [128, 16, 6], F32)
        mv = sb("mv", [128, 16, 2], F32)
        rs = sb("rs", [128, 16], F32)
        rsl = sb("rsl", [128, B], F32)
        zl = sb("zl", [128, B, 2, 128], F16)
        zlT = sb("zlT", [128, 2, B, 128], F16)
        zc = sb("zc", [128, B * NC, 2, 128], F16)
        zcT = sb("zcT", [128, B * NC, 2, 128], F16)
        raw = sb("raw", [128, 2, NC, 128], F32)
        qq = sb("qq", [128, 2, 2, B, QB], F16)
        reg = sb("reg", [128, 9216], F32)
        wq_s = reg[:, 0:1024]
        wkv_s = reg[:, 1024:3072]
        wkT = [reg[:, 3072 + 1024 * k:4096 + 1024 * k].bitcast(F16)
               .rearrange("p (j t a) -> p j t a", j=NJ, t=2) for k in range(2)]
        qT = [reg[:, 5120 + 2048 * k:7168 + 2048 * k].bitcast(F16)
              .rearrange("p (j n) -> p j n", j=NJ) for k in range(2)]
        wqt = zc[:].rearrange("p u a k -> p (u a k)")[:, 0:2 * INNER].rearrange("p (a n) -> p a n", a=2)
        p32 = reg[:, 0:1024].rearrange("p (j n) -> p j n", j=2)
        ph = reg[:, 1024:1536].bitcast(F16).rearrange("p (j n) -> p j n", j=2)
        pl = reg[:, 1536:2048].bitcast(F16).rearrange("p (j n) -> p j n", j=2)
        th = reg[:, 2048:3072].bitcast(F16).rearrange("p (t n) -> p t n", t=2)
        tl = reg[:, 3072:4096].bitcast(F16).rearrange("p (t n) -> p t n", t=2)
        on = reg[:, 4096:4608].rearrange("p (h d) -> p h d", h=HG)
        oT = reg[:, 4608:5632].rearrange("p (j n) -> p j n", j=NJ)
        mrun = reg[:, 7168:9216]
        rinv = sb("rinv", [128, HG], F32)
        wv = sb("wv", [128, 2, 2, H, DH + 1], F16)
        cm = sb("cm", [128, 2, NJ, 2, 2], F16)
        wo_s = sb("wo_s", [128, NJ, D], F32)
        c32 = sb("c32", [128, B, 2, H], F32)
        mall = sb("mall", [128, H], F32)
        r32 = sb("r32", [128, 2, H], F32)
        rhl = sb("rhl", [128, 2, 2, H], F16)
        rT = sb("rT", [64, 128], F16)
        rawflat = raw[:].rearrange("p s c k -> p (s c k)")
        w1_s = rawflat[:, 0:E * F2].rearrange("p (e f) -> p e f", e=E)
        aw = rawflat[:, 2816:3328].rearrange("p (k n) -> p k n", k=4)
        abr = rawflat[:, 3328:3584].rearrange("p (k n) -> p k n", k=2)
        rw_s = rawflat[:, 3584:3592]
        ab = rawflat[:, 3592:3594]
        late = qq[:].rearrange("p a t b n -> p (a t b n)").bitcast(F32)
        xT = late[:, 0:512]
        qTa = late[:, 512:1024]
        kTa = late[:, 1024:1536]
        kblk = late[:, 1536:3584].rearrange("p (b h k) -> p b h k", b=B, h=4)
        va = late[:, 3584:4160].rearrange("p (b h d) -> p b h d", b=B, h=AH)
        amax = late[:, 4160:4224].rearrange("p (b h) -> p b h", b=B)
        nmax = late[:, 4224:4288].rearrange("p (b h) -> p b h", b=B)
        pa = late[:, 4288:6336].rearrange("p (h k) -> p h k", h=AH)
        paT = late[:, 6336:8384].rearrange("p (h k) -> p h k", h=AH)
        ra = late[:, 8384:8400]
        oa = late[:, 8400:8528]
        oaT = late[:, 8528:8656]
        lg = late[:, 8656:8688].rearrange("p (b e) -> p b e", b=B)
        lgm = late[:, 8688:8692]
        ex = late[:, 8692:8724].rearrange("p (b e) -> p b e", b=B)
        sm = late[:, 8724:8728]
        gtm = late[:, 8728:8984].rearrange("p (b f) -> p b f", f=E)
        eqm = late[:, 8984:9240].rearrange("p (b f) -> p b f", f=E)
        rank = late[:, 9240:9272]
        pr = late[:, 9272:9304].rearrange("p (b e) -> p b e", b=B)
        tt = late[0:FH, 9304:10328].rearrange("p (k n) -> p k n", k=2)
        gg = late[0:FH, 10328:11352].rearrange("p (k n) -> p k n", k=2)
        w2_s = reg[0:FH, 7168:9216].rearrange("p (c d) -> p c d", c=2 * E)
        gT = zc[:].rearrange("p u a k -> p (u a k)").bitcast(F32)[:, 0:8192].rearrange(
            "p (c n) -> p c n", c=2 * E)

        names = """mask_in x_in gb_in wkv_in wq_in wo_in late_in ctx_in0 ctx_in1 const_done
            pool_fold fl_done cnt_done meta_done mb_done seq gt_done stat_ready rs_ready
            lat_ready latT_done fill hi lo c_done c_used ctx_stat ctx_rs z_ready zT_fill zT_copied
            slab_free q_scores q_max r_ready rT_done rT_copied row_set
            sc_ready exp_done p_ready pv_done t_ready t_hi t_lo u_done on_ready oT_fill oT_copied
            xo_done x1_done
            xT_fill xT_done ctx_bn ctx_ag z_full z_hi r_seq p_hi u_inv passed_dve passed_sp passed_pe passed_act a_fill a_done a_s a_max a_exp a_tr a_trc a_pv a_o a_oT a_oTc a_y a_x2
            r_log r_exp f_y f_t f_g f_o f_acc out_sent ready_out pre""".split()
        s = {n: sem(n) for n in names}

        mask_rows = mask.rearrange("b (c k) -> (b c) k", c=NC)
        x_rows = x.rearrange("b l d -> l b d")
        out_rows = out.rearrange("b l d -> l b d")
        ctx_rows = ctxt.rearrange("b (c k) d -> b c k d", c=NC)

        T_WK, T_WQ, T_WV, T_QT, T_QQ = 0, 4, 6, 10, 18
        N_FILL = T_QQ + 2 * H
        block = ctx.enter_context(nc.Block())

        def load_counts(eng, b):
            n = eng.value_load(meta[0:1, bass.ds(b, 1)], min_val=2, max_val=NC)
            off = eng.value_load(meta[0:1, bass.ds(b + 4, 1)], min_val=0, max_val=3 * NC)
            return n, off

        def prepared(e, part):
            src = ps[:, e % 8, :]
            if e < T_WQ:
                return wkT[part][:, 2 * e:2 * e + 2, :, :].rearrange("p j t a -> p (j t a)"), src
            if e < T_WV:
                k = (e - T_WQ) * 512
                return wqt[:, part, k:k + 512], src
            if e < T_QT:
                t, k = (e - T_WV) // 2, (e - T_WV) % 2 * 8
                return wv[:, part, t, k:k + 8, 0:DH], src.rearrange("p (h d) -> p h d", h=8)
            if e < T_QQ:
                return qT[part][:, e - T_QT, :], src
            h, t = (e - T_QQ) // 2, (e - T_QQ) % 2
            return qq[:, part, t, :, h * 128:h * 128 + 128], src.rearrange("p (b l) -> p b l", b=B)

        @block.sync
        def _(sp):
            sp.dma_start(mk[:], mask_rows).then_inc(s["mask_in"], 16)
            sp.dma_start(xs[:], x_rows).then_inc(s["x_in"], 16)
            for k, v in enumerate((g1, b1, g2, b2)):
                sp.dma_start(gb[:, k:k + 1], v.rearrange("(p o) -> p o", o=1)).then_inc(s["gb_in"], 16)
            sp.dma_start(wkv_s, Wkv).then_inc(s["wkv_in"], 16)
            sp.dma_start(wq_s, Wq).then_inc(s["wq_in"], 16)
            sp.dma_start(wo_s[:], Wout.rearrange("(j p) d -> p j d", p=128)).then_inc(s["wo_in"], 16)
            sp.wait_ge(s["meta_done"], 1)
            with sp.Fori(0, B // 2) as pair:
                for par in range(2):
                    b = 2 * pair + par
                    n = sp.value_load(meta[0:1, bass.ds(b, 1)], min_val=2, max_val=NC)
                    sp.wait_ge(s["slab_free"], b + 1)
                    sp.sem_inc(s["passed_sp"], 1)
                    with sp.Fori(0, n) as i:
                        sp.dma_start(raw[:, par, bass.ds(i, 1), :].rearrange("p o d -> p (o d)"),
                                     ctx_rows[bass.ds(b, 1), bass.ds(NC - 1 - i, 1), :, :]
                                     .rearrange("a c k d -> (a c k) d")).then_inc(s[f"ctx_in{par}"], 16)
            sp.wait_ge(s["slab_free"], B + 2)
            sp.dma_start(w1_s, w1.rearrange("e h f -> h e f")).then_inc(s["late_in"], 16)
            sp.wait_ge(s["r_ready"], B)
            sp.dma_start(w2_s, w2.rearrange("e (c f) d -> f (e c) d", c=2)).then_inc(s["late_in"], 16)
            sp.dma_start(rw_s, rw).then_inc(s["late_in"], 16)
            for k, w in enumerate((aWq, aWk, aWv, aWo)):
                sp.dma_start(aw[:, k, :], w).then_inc(s["late_in"], 16)
            for k, v in enumerate((abq, abk)):
                sp.dma_start(ab[:, k:k + 1], v.rearrange("(p o) -> p o", o=1)).then_inc(s["late_in"], 16)
            for k, v in enumerate((abv, abo)):
                sp.dma_start(abr[:, k, :], v.rearrange("(o d) -> o d", o=1).broadcast_to([128, 128])
                             ).then_inc(s["late_in"], 16)
            sp.wait_ge(s["ready_out"], 1)
            sp.dma_start(out_rows, xs[:]).then_inc(s["out_sent"], 16)
            sp.wait_ge(s["out_sent"], 16)
        LATE = 16 * 11

        @block.gpsimd
        def _(pool):
            order = [0]

            def link(ins):
                order[0] += 1
                ins.then_inc(s["const_done"], 1)
                pool.wait_ge(s["const_done"], order[0])

            link(pool.memset(ident[:], 0.0))
            link(pool.affine_select(out=ident[:], in_=ident[:], compare_op=ALU.not_equal, fill=1.0,
                                    base=0, pattern=[[-1, 128]], channel_multiplier=1))
            link(pool.iota(weight[:].rearrange("p (b c) -> p b c", b=B), [[0, B], [-1, NC]], base=NC,
                           channel_multiplier=0, allow_small_or_imprecise_dtypes=True))
            link(pool.affine_select(out=fold[:], in_=ident[:], compare_op=ALU.not_equal, fill=-1.0,
                                    base=-127, pattern=[[0, 128]], channel_multiplier=1))
            link(pool.tensor_copy(identh[:], ident[:]))
            link(pool.memset(neghalf[:], -0.5))
            pool.memset(zero2[:], 0.0).then_inc(s["pool_fold"], 1)
            for k in range(2):
                pool.wait_ge(s["stat_ready"], k + 1)
                pool.tensor_tensor(rsl[:], rsl[:], neghalf[:, 0:B], ALU.pow).then_inc(s["rs_ready"], 1)
            pool.memset(wv[:], 0.0).then_inc(s["pool_fold"], 1)
            pool.wait_ge(s["pool_fold"], 2)
            for t in range(2):
                pool.affine_select(out=wv[:, 0, t, :, DH], in_=wv[:, 0, t, :, DH],
                                   compare_op=ALU.not_equal, fill=1.0, base=-127, pattern=[[0, H]],
                                   channel_multiplier=1).then_inc(s["pool_fold"], 1)
            with pool.Fori(0, B) as b:
                pool.wait_ge(s["ctx_stat"], b + 1)
                pool.tensor_tensor(rs[:], rs[:], neghalf[:, 0:16], ALU.pow).then_inc(s["ctx_rs"], 1)
            link(pool.memset(band[:], 0.0))
            link(pool.affine_select(out=band[:], in_=band[:], compare_op=ALU.is_ge, fill=OUTSIDE,
                                    base=WINDOW // 2, pattern=[[-1, 128]], channel_multiplier=1))
            link(pool.affine_select(out=band[:], in_=band[:], compare_op=ALU.is_ge, fill=OUTSIDE,
                                    base=WINDOW // 2, pattern=[[1, 128]], channel_multiplier=-1))
            link(pool.tensor_copy(identb[:], ident[:]))
            link(pool.memset(headmask[:], 0.0))
            for g in range(4):
                sub = headmask[32 * g:32 * g + 32, :]
                link(pool.memset(sub, 1.0))
                link(pool.affine_select(out=sub, in_=sub, compare_op=ALU.is_ge, fill=0.0, base=0,
                                        pattern=[[-DK, 4]], channel_multiplier=1))
                link(pool.affine_select(out=sub, in_=sub, compare_op=ALU.is_ge, fill=0.0, base=DK - 1,
                                        pattern=[[DK, 4]], channel_multiplier=-1))
            link(pool.memset(tri[:], 1.0))
            link(pool.affine_select(out=tri[:], in_=tri[:], compare_op=ALU.is_gt, fill=0.0, base=0,
                                    pattern=[[1, E], [-1, E]], channel_multiplier=0))
            for k in range(2):
                pool.wait_ge(s["stat_ready"], k + 3)
                pool.tensor_tensor(rsl[:], rsl[:], neghalf[:, 0:B], ALU.pow).then_inc(s["rs_ready"], 1)
        N_CONST = 6 + 5 + 12 + 2

        @block.tensor
        def _(pe):
            def bank(k):
                return ps[:, k % 8, :]

            pe.wait_ge(s["const_done"], 5)
            pe.wait_ge(s["fl_done"], 2)
            pe.matmul(ps[0:1, 6, 0:64], flag[:], ident[0:64, 0:64], start=True, stop=True)
            pe.transpose(ps[:, 7, 0:64], mkf[:], ident[0:64, 0:64]).then_inc(s["cnt_done"], 1)
            pe.wait_ge(s["lat_ready"], 1)
            tp = ps[:, 5, :].bitcast(F16)
            for hl in range(2):
                for b in range(B):
                    mm = pe.transpose(tp[:, (hl * B + b) * 128:(hl * B + b + 1) * 128], zl[:, b, hl, :], identh[:])
            mm.then_inc(s["latT_done"], 1)
            pe.wait_ge(s["gt_done"], 1)
            pe.wait_ge(s["wkv_in"], 16)
            for k in range(4):
                for q in range(2):
                    j = 2 * k + q
                    mm = pe.matmul(bank(k)[:, q * 256:q * 256 + 256], wkv_s[:, j * 128:j * 128 + 128],
                                   gt[:].rearrange("p t a -> p (t a)"), start=True, stop=True)
                mm.then_inc(s["fill"], 1)
            pe.wait_ge(s["wq_in"], 16)
            for k in range(2):
                if k == 1:
                    pe.wait_ge(s["latT_done"], 2)
                pe.matmul(bank(T_WQ + k), gt[:, 1, :], wq_s[:, k * 512:k * 512 + 512],
                          start=True, stop=True).then_inc(s["fill"], 1)
            pe.wait_ge(s["meta_done"], 1)
            pe.wait_ge(s["mb_done"], 1)
            for t in range(2):
                for k in range(2):
                    e = T_WV + 2 * t + k
                    if e >= 8:
                        pe.wait_ge(s["lo"], e - 7)
                    pe.matmul(bank(e), gt[:, t, :], wkv_s[:, INNER + k * 512:INNER + k * 512 + 512],
                              start=True, stop=True).then_inc(s["fill"], 1)

            def three(dst, a, b, ah, al, bh, bl):
                pe.matmul(dst, ah, bh, start=True, stop=False)
                pe.matmul(dst, ah, bl, start=False, stop=False)
                return pe.matmul(dst, al, bh, start=False, stop=True)

            latT = [zlT[:, k, :, :].rearrange("p b l -> p (b l)") for k in range(2)]
            for j in range(NJ):
                e = T_QT + j
                pe.wait_ge(s["lo"], max(e - 7, T_WV))
                w = [wqt[:, k, j * 128:j * 128 + 128] for k in range(2)]
                three(bank(e), None, None, w[0], w[1], latT[0], latT[1]).then_inc(s["fill"], 1)
            for h in range(H):
                j, r = h // 2, 64 * (h % 2)
                for t in range(2):
                    e = T_QQ + 2 * h + t
                    pe.wait_ge(s["lo"], max(e - 7, T_QT + j + 1))
                    w = [wkT[k][r:r + 64, j, t, :] for k in range(2)]
                    q = [qT[k][r:r + 64, j, :] for k in range(2)]
                    three(bank(e), None, None, w[0], w[1], q[0], q[1]).then_inc(s["fill"], 1)
            pe.wait_ge(s["lo"], N_FILL)
            pe.wait_ge(s["c_used"], 4)
            for b in range(B):
                for j in range(NJ):
                    for k in range(3):
                        lhs = qT[1 if k == 1 else 0][:, j, b * 128:b * 128 + 128]
                        mm = pe.matmul(ps[:, 0, b * 32 + 4 * j:b * 32 + 4 * j + 4], lhs,
                                       cm[:, 1 if k == 2 else 0, j, :, :].rearrange("p t r -> p (t r)"), start=(k == 0), stop=(k == 2))
            mm.then_inc(s["c_done"], 1)

            with pe.Fori(0, B) as b:
                n, off = load_counts(pe, b)
                with pe.Fori(0, n) as i:
                    u = off + i
                    pe.wait_ge(s["z_ready"], u + 1)
                    pe.wait_ge(s["zT_copied"], u + 1)
                    for hl in range(2):
                        mm = pe.transpose(ps[:, 5, :].bitcast(F16)[:, hl * 128:hl * 128 + 128],
                                          zc[:, bass.ds(u, 1), hl, :].rearrange("p o d -> p (o d)"), identh[:])
                    mm.then_inc(s["zT_fill"], 1)

            with pe.Fori(0, B) as b:
                n, off = load_counts(pe, b)
                base = off + 2 * b

                def fast(zT, t, u):
                    for half in range(2):
                        pe.wait_ge(s["q_max"], 2 * u + half + 1)
                        for k in range(2):
                            c = (2 * half + k) * 512
                            mm = pe.matmul(ps[:, 1 + 2 * half + k, :], zT,
                                           qq[:, 0, t, bass.ds(b, 1), c:c + 512].rearrange("p o n -> p (o n)"),
                                           start=True, stop=True)
                        mm.then_inc(s["q_scores"], 1)

                fast(zlT[:, 0, bass.ds(b, 1), :].rearrange("p o d -> p (o d)"), 1, base)
                with pe.Fori(0, n) as i:
                    pe.wait_ge(s["zT_copied"], off + i + 2)
                    fast(zcT[:, bass.ds(off + i, 1), 0, :].rearrange("p o d -> p (o d)"), 0, base + i + 1)
                for half in range(2):
                    pe.wait_ge(s["q_max"], 2 * (base + n + 1) + 2)
                    for k in range(8):
                        c = (8 * half + k) * 128
                        mm = pe.transpose(ps[:, 1 + 2 * half + k // 4, (k % 4) * 128:(k % 4) * 128 + 128],
                                          mrun[:, c:c + 128], ident[:])
                    mm.then_inc(s["q_scores"], 1)
                pe.wait_ge(s["r_ready"], b + 1)
                pe.wait_ge(s["rT_copied"], b + 1)
                pe.sem_inc(s["passed_pe"], 1)
                pe.transpose(ps[0:64, 6, :].bitcast(F16)[:, 0:128],
                             rhl[:].rearrange("p a t h -> p (a t h)"), identh[:]).then_inc(s["rT_done"], 1)

            SC, T1, T2, UB = 0, 2, 4, 6
            with pe.Fori(0, B) as b:
                n, off = load_counts(pe, b)
                pe.wait_ge(s["row_set"], 64 * b + 128)
                for g in range(2):
                    base = 2 * (off + b) + g * (n + 1)

                    def scores(zT, t, u):
                        for k in range(2):
                            pe.wait_ge(s["exp_done"], 2 * u + k + 1)
                            c = g * GC + k * 512
                            rhs = [qq[:, a, t, bass.ds(b, 1), c:c + 512].rearrange("p o n -> p (o n)")
                                   for a in range(2)]
                            three(ps[:, SC + k, :], None, None, zT[0], zT[1], rhs[0], rhs[1]
                                  ).then_inc(s["sc_ready"], 1)

                    def values(z, dst, u, first, last=None):
                        for k in range(2):
                            pe.wait_ge(s["p_ready"], 2 * u + k + 3)
                            d = ps[:, dst + k, :]
                            pe.matmul(d, z[0], ph[:, k, :], start=first, stop=False, skip_group_check=True)
                            pe.matmul(d, z[0], pl[:, k, :], start=False, stop=False, skip_group_check=True)
                            mm = pe.matmul(d, z[1], ph[:, k, :], start=False, stop=first, skip_group_check=True)
                            mm.then_inc(s["pv_done"], 1)

                    def at(tile, hl, idx):
                        if tile is zlT:
                            return tile[:, hl, bass.ds(idx, 1), :].rearrange("p o d -> p (o d)")
                        return tile[:, bass.ds(idx, 1), hl, :].rearrange("p o d -> p (o d)")

                    scores([at(zlT, 0, b), at(zlT, 1, b)], 1, base)
                    scores([at(zcT, 0, off), at(zcT, 1, off)], 0, base + 1)
                    pe.wait_ge(s["t_lo"], 2 * (2 * b + g) + 2)
                    values([at(zl, 0, b), at(zl, 1, b)], T2, base, True)
                    for k in range(2):
                        pe.matmul(ps[:, T1 + k, 0:2], zero2[:, 0:128], zero2[:, 128:130],
                                  start=True, stop=False, skip_group_check=True)
                    with pe.Fori(1, n) as i:
                        scores([at(zcT, 0, off + i), at(zcT, 1, off + i)], 0, base + i + 1)
                        values([at(zc, 0, off + i - 1), at(zc, 1, off + i - 1)], T1, base + i, False)
                    values([at(zc, 0, off + n - 1), at(zc, 1, off + n - 1)], T1, base + n, False)

                    pe.wait_ge(s["t_lo"], 2 * (2 * b + g) + 4)
                    pe.wait_ge(s["oT_copied"], 2 * b + g + 1)
                    pe.wait_ge(s["x1_done"], b + 1)
                    for h in range(HG):
                        o = ps[:, UB + h // 4, (h % 4) * (DH + 1):(h % 4 + 1) * (DH + 1)]
                        c = h * 128
                        step = 0
                        for t in range(2):
                            for a, w in ((th, 0), (th, 1), (tl, 0)):
                                mm = pe.matmul(o, a[:, t, c:c + 128], wv[:, w, t, g * HG + h, :],
                                               start=(step == 0), stop=(step == 5))
                                step += 1
                    mm.then_inc(s["u_done"], 1)
                    pe.wait_ge(s["on_ready"], 2 * b + g + 1)
                    for k in range(4):
                        mm = pe.transpose(ps[:, UB, k * 128:k * 128 + 128],
                                          on[:, 2 * k:2 * k + 2, :].rearrange("p h d -> p (h d)"), ident[:])
                    mm.then_inc(s["oT_fill"], 1)
                pe.wait_ge(s["oT_copied"], 2 * b + 3)
                for j in range(NJ):
                    mm = pe.matmul(ps[:, UB + 1, 0:128], oT[:, j, :], wo_s[:, j, :],
                                   start=(j == 0), stop=(j == NJ - 1))
                mm.then_inc(s["xo_done"], 1)

            def turn_norm(k):
                pe.wait_ge(s["lat_ready"], k + 2)
                for b in range(B):
                    mm = pe.transpose(ps[:, 0, b * 128:b * 128 + 128], xn[:, b, :], ident[:])
                mm.then_inc(s["xT_fill"], 1)
                pe.wait_ge(s["xT_done"], k + 1)

            pe.wait_ge(s["late_in"], LATE)
            pe.wait_ge(s["const_done"], N_CONST)
            turn_norm(0)
            pe.matmul(ps[:, 1, :], aw[:, 0, :], xT, start=True, stop=True)
            pe.matmul(ps[:, 2, :], aw[:, 1, :], xT, start=True, stop=True)
            for b in range(B):
                mm = pe.matmul(ps[:, 3, b * 128:b * 128 + 128], xT[:, b * 128:b * 128 + 128], aw[:, 2, :],
                               start=True, stop=True)
            mm.then_inc(s["a_fill"], 1)
            pe.wait_ge(s["a_done"], 1)
            for b in range(B):
                if b >= 1:
                    pe.wait_ge(s["a_exp"], b)
                for g in range(4):
                    d = ps[:, g, :]
                    pe.matmul(d, qTa[32 * g:32 * g + 32, b * 128:b * 128 + 128],
                              kblk[32 * g:32 * g + 32, b, :, :].rearrange("p h k -> p (h k)"),
                              start=True, stop=False)
                    mm = pe.matmul(d, identb[:], band[:, None, :].broadcast_to([128, 4, 128]), start=False, stop=True)
                mm.then_inc(s["a_s"], 1)
                pe.wait_ge(s["a_exp"], b + 1)
                for g in range(2):
                    if g == 1 or b >= 1:
                        pe.wait_ge(s["a_trc"], 2 * b + g)
                    for k in range(8):
                        h = 8 * g + k
                        mm = pe.transpose(ps[:, 4 + k // 4, (k % 4) * 128:(k % 4) * 128 + 128], pa[:, h, :], ident[:])
                    mm.then_inc(s["a_tr"], 1)
                pe.wait_ge(s["a_trc"], 2 * b + 2)
                for h in range(AH):
                    mm = pe.matmul(ps[:, 6, 9 * h:9 * h + 9], paT[:, h, :], va[:, b, h, :], start=True, stop=True)
                mm.then_inc(s["a_pv"], 1)
                pe.wait_ge(s["a_o"], b + 1)
                pe.transpose(ps[:, 7, 0:128], oa, ident[:]).then_inc(s["a_oT"], 1)
                pe.wait_ge(s["a_oTc"], b + 1)
                pe.matmul(ps[:, 7, 128:256], oaT, aw[:, 3, :], start=True, stop=True).then_inc(s["a_y"], 1)
                pe.wait_ge(s["a_x2"], b + 1)

            turn_norm(1)
            for b in range(B):
                mm = pe.matmul(ps[:, 1, b * E:b * E + E], xT[:, b * 128:b * 128 + 128], rw_s, start=True, stop=True)
            mm.then_inc(s["r_log"], 1)
            for c in range(2 * E):
                e, half = c // 2, c % 2
                if c >= 2:
                    pe.wait_ge(s["f_g"], c - 1)
                for k in range(2):
                    w = w1_s[:, e, k * F + half * FH:k * F + half * FH + FH]
                    mm = pe.matmul(ps[0:FH, 2 + 2 * (c % 2) + k, :], w, xT, start=True, stop=True)
                mm.then_inc(s["f_y"], 1)
            pe.wait_ge(s["f_g"], 2 * E)
            for b in range(B):
                for q in range(2):
                    d = 2 * b + q
                    if d >= 2:
                        pe.wait_ge(s["f_acc"], d - 1)
                    for k in range(4):
                        e = 4 * q + k
                        for half in range(2):
                            mm = pe.matmul(ps[:, 6 + q, k * 128:k * 128 + 128],
                                           gT[0:FH, 2 * e + half, b * 128:b * 128 + 128], w2_s[:, 2 * e + half, :],
                                           start=(half == 0), stop=(half == 1))
                    mm.then_inc(s["f_o"], 1)

        @block.scalar
        def _(act):
            act.sem_inc(s["zT_copied"], 1)
            act.sem_inc(s["rT_copied"], 1)
            act.sem_inc(s["row_set"], 64)
            act.sem_inc(s["exp_done"], 2)
            act.sem_inc(s["oT_copied"], 1)

            def copy(o, i):
                return act.activation(o, i, ACT.Copy)

            act.wait_ge(s["latT_done"], 1)
            copy(zlT[:].rearrange("p a b l -> p (a b l)"), ps[:, 5, :].bitcast(F16)).then_inc(s["latT_done"], 1)
            for e in range(N_FILL):
                act.wait_ge(s["fill"], e + 1)
                if e == T_WV:
                    act.wait_ge(s["pool_fold"], 4)
                copy(*prepared(e, 0)).then_inc(s["hi"], 1)
            with act.Fori(0, B) as b:
                n, off = load_counts(act, b)
                with act.Fori(0, n) as i:
                    act.wait_ge(s["zT_fill"], off + i + 1)
                    act.sem_inc(s["passed_act"], 1)
                    copy(zcT[:, bass.ds(off + i, 1), :, :].rearrange("p o a k -> p (o a k)"),
                         ps[:, 5, :].bitcast(F16)[:, 0:256]).then_inc(s["zT_copied"], 1)
            with act.Fori(0, B) as b:
                act.wait_ge(s["rT_done"], b + 2)
                act.wait_ge(s["row_set"], 64 * b + 64)
                copy(rT[:], ps[0:64, 6, :].bitcast(F16)[:, 0:128]).then_inc(s["rT_copied"], 1)
                act.wait_ge(s["rT_copied"], b + 2)
                for k in range(4):
                    act.dma_start(qq[127:128, k // 2, k % 2, bass.ds(b, 1), :].rearrange("p o (h l) -> p (o h) l", h=H),
                                  rT[H * k:H * k + H, :]).then_inc(s["row_set"], 16)

            with act.Fori(0, B) as b:
                n, off = load_counts(act, b)
                for g in range(2):
                    base = 2 * (off + b) + g * (n + 1)

                    def exps(u, bias):
                        for k in range(2):
                            act.wait_ge(s["sc_ready"], 2 * u + k + 1)
                            act.wait_ge(s["p_ready"], 2 * u + k + 1)
                            act.sem_inc(s["passed_act"], 1)
                            act.activation(p32[:, k, :], ps[:, k, :], ACT.Exp, bias=bias, scale=XSCALE
                                           ).then_inc(s["exp_done"], 1)

                    def sums(t, u, count):
                        act.wait_ge(s["pv_done"], 2 * u + 4)
                        if count == 1:
                            act.wait_ge(s["u_done"], 2 * b + g + 1)
                        act.activation(th[:, t, :], ps[:, 2 + 2 * t:4 + 2 * t, :].rearrange("p k n -> p (k n)"),
                                       ACT.Copy, scale=TSCALE).then_inc(s["t_hi"], 1)

                    exps(base, 0.0)
                    exps(base + 1, mbias[:, bass.ds(NC * b + NC - 1, 1)])
                    sums(1, base, 1)
                    with act.Fori(1, n) as i:
                        exps(base + i + 1, mbias[:, bass.ds(NC * b + NC - 1 - i, 1)])
                    sums(0, base + n, 2)
                    act.wait_ge(s["oT_fill"], 2 * b + g + 2)
                    act.wait_ge(s["xo_done"], b + 1)
                    copy(oT[:, 4 * g:4 * g + 4, :].rearrange("p j n -> p (j n)"), ps[:, 6, :]
                         ).then_inc(s["oT_copied"], 1)

            act.wait_ge(s["xT_fill"], 1)
            copy(xT, ps[:, 0, :]).then_inc(s["xT_done"], 1)
            for b in range(B):
                act.wait_ge(s["a_max"], b + 1)
                if b >= 1:
                    act.wait_ge(s["a_tr"], 2 * b)
                for h in range(AH):
                    ins = act.activation(pa[:, h, :], ps[:, h // 4, (h % 4) * 128:(h % 4) * 128 + 128], ACT.Exp,
                                         bias=nmax[:, b, h:h + 1], scale=ASCALE)
                ins.then_inc(s["a_exp"], 1)
                act.wait_ge(s["a_oT"], b + 1)
                if b >= 1:
                    act.wait_ge(s["a_y"], b)
                copy(oaT, ps[:, 7, 0:128]).then_inc(s["a_oTc"], 1)
            act.wait_ge(s["xT_fill"], 2)
            copy(xT, ps[:, 0, :]).then_inc(s["xT_done"], 1)
            act.wait_ge(s["r_log"], 2)
            act.activation(ex[:].rearrange("p b e -> p (b e)"), lg[:].rearrange("p b e -> p (b e)"), ACT.Exp
                           ).then_inc(s["r_exp"], 1)
            for c in range(2 * E):
                act.wait_ge(s["f_y"], c + 1)
                if c >= 2:
                    act.wait_ge(s["f_g"], c - 1)
                act.activation(tt[:, c % 2, :], ps[0:FH, 2 + 2 * (c % 2), :], ACT.Tanh, scale=0.5
                               ).then_inc(s["f_t"], 1)

        @block.vector
        def _(dve):
            dve.sem_inc(s["slab_free"], 2)
            dve.sem_inc(s["q_max"], 2)
            dve.sem_inc(s["rT_done"], 1)
            dve.sem_inc(s["p_ready"], 2)
            dve.sem_inc(s["pv_done"], 2)
            dve.sem_inc(s["t_lo"], 2)
            dve.sem_inc(s["u_done"], 1)
            dve.sem_inc(s["x1_done"], 1)
            dve.sem_inc(s["xo_done"], 1)
            dve.sem_inc(s["oT_fill"], 1)
            order = [0]

            def link(ins):
                order[0] += 1
                ins.then_inc(s["seq"], 1)
                dve.wait_ge(s["seq"], order[0])

            def norm(src, k):
                for b in range(B):
                    ins = dve.bn_stats(st[:, b, :], src[:, b, :])
                link(ins)
                for b in range(B):
                    ins = dve.bn_aggr(mv[:, b, :], st[:, b, :])
                link(ins)
                dve.tensor_scalar(rsl[:], mv[:, 0:B, 1], EPS, None, ALU.add).then_inc(s["stat_ready"], 1)
                dve.wait_ge(s["rs_ready"], k + 1)
                for b in range(B):
                    ins = dve.tensor_scalar(xn[:, b, :], src[:, b, :], mv[:, b, 0:1], rsl[:, b:b + 1],
                                            ALU.subtract, ALU.mult)
                return ins

            dve.memset(rs[:], 1.0)
            dve.memset(mv[:], 1.0)
            dve.memset(st[:], 1.0)
            dve.memset(metaf[:], 0.0)
            dve.wait_ge(s["mask_in"], 16)
            dve.tensor_copy(mkf[:], mk[:]).then_inc(s["fl_done"], 1)
            dve.wait_ge(s["fl_done"], 1)
            dve.tensor_reduce(flag[:], mkf[:], AX_X, ALU.max).then_inc(s["fl_done"], 1)
            dve.wait_ge(s["cnt_done"], 1)
            dve.tensor_scalar(mbias[:], ps[:, 7, 0:64], 1.0, -MASKED, ALU.subtract, ALU.mult).then_inc(s["mb_done"], 1)
            link(dve.tensor_tensor(lastc[:], ps[0:1, 6, 0:64], weight[:], ALU.mult))
            link(dve.tensor_reduce(metaf[:, 0:4], lastc[:].rearrange("p (b c) -> p b c", b=B), AX_X, ALU.max))
            link(dve.tensor_scalar(metaf[:, 0:4], metaf[:, 0:4], 2.0, None, ALU.max))
            dve.tensor_copy(metaf[:, 5:6], metaf[:, 0:1])
            dve.tensor_tensor(metaf[:, 6:7], metaf[:, 0:1], metaf[:, 1:2], ALU.add)
            dve.tensor_copy(metaf[:, 8:10], metaf[:, 0:2])
            link(dve.tensor_tensor(metaf[:, 10:12], metaf[:, 0:2], metaf[:, 2:4], ALU.add))
            link(dve.tensor_tensor(metaf[:, 7:8], metaf[:, 10:11], metaf[:, 1:2], ALU.add))
            dve.tensor_copy(meta[:], metaf[:]).then_inc(s["meta_done"], 1)

            dve.wait_ge(s["x_in"], 16)
            link(norm(xs, 0))
            link(norm(xn, 1))
            link(dve.memset(xn[:, :, 127:128], 1.0))
            xnf = xn[:]
            link(dve.tensor_copy(zl[:, :, 0, :], xnf))
            dve.tensor_tensor(zl[:, :, 1, :], xnf, zl[:, :, 0, :], ALU.subtract).then_inc(s["lat_ready"], 1)

            dve.wait_ge(s["const_done"], 5)
            dve.wait_ge(s["gb_in"], 64)
            for t in range(2):
                dve.tensor_scalar(gt[:, t, 0:127], fold[:, 0:127], gb[:, 2 * t:2 * t + 1], None, ALU.mult)
                ins = dve.tensor_copy(gt[:, t, 127:128], gb[:, 2 * t + 1:2 * t + 2])
            ins.then_inc(s["gt_done"], 1)
            dve.memset(cm[:], 0.0)

            for e in range(N_FILL):
                dve.wait_ge(s["hi"], e + 1)
                o, i = prepared(e, 1)
                dve.tensor_tensor(o, i, prepared(e, 0)[0], ALU.subtract).then_inc(s["lo"], 1)
                if e == T_WK + 3:
                    dve.wait_ge(s["lo"], e + 1)
                    for k in range(2):
                        for r in range(2):
                            dve.tensor_copy(cm[64 * r:64 * r + 64, k, :, :, r],
                                            wkT[k][64 * r:64 * r + 64, :, :, 127]).then_inc(s["c_used"], 1)
            dve.wait_ge(s["c_done"], 1)
            for t in range(2):
                ins = dve.tensor_copy(c32[:, :, t, :].rearrange("p b (j r) -> p b j r", r=2),
                                      ps[:, 0, 0:128].rearrange("p (b j t r) -> p b j t r", b=B, j=NJ, t=2)[:, :, :, t, :])
            link(ins)

            dve.wait_ge(s["meta_done"], 1)
            with dve.Fori(0, B // 2) as pair:
                for par in range(2):
                    b = 2 * pair + par
                    n, off = load_counts(dve, b)
                    loads = dve.value_load(meta[0:1, bass.ds(b + 8, 1)], min_val=2, max_val=2 * NC)
                    dve.wait_ge(s[f"ctx_in{par}"], 16 * loads)
                    dve.sem_inc(s["passed_dve"], 1)
                    with dve.Fori(0, n) as i:
                        row = raw[:, par, bass.ds(i, 1), :].rearrange("p o k -> p (o k)")
                        dve.bn_stats(st[:, bass.ds(i, 1), :].rearrange("p o k -> p (o k)"), row
                                     ).then_inc(s["ctx_bn"], 1)
                    dve.wait_ge(s["ctx_bn"], off + n)
                    dve.sem_inc(s["passed_dve"], 1)
                    for k in range(NC):
                        ins = dve.bn_aggr(mv[:, k, :], st[:, k, :])
                    ins.then_inc(s["ctx_ag"], 1)
                    dve.wait_ge(s["ctx_ag"], 2 * b + 1)
                    dve.memset(raw[:, par, :, 127:128], 1.0).then_inc(s["ctx_ag"], 1)
                    dve.tensor_scalar(rs[:], mv[:, :, 1], EPS, None, ALU.add).then_inc(s["ctx_stat"], 1)
                    dve.wait_ge(s["ctx_ag"], 2 * b + 2)
                    dve.wait_ge(s["ctx_rs"], b + 1)
                    dve.sem_inc(s["passed_dve"], 1)
                    with dve.Fori(0, n) as i:
                        row = raw[:, par, bass.ds(i, 1), :].rearrange("p o k -> p (o k)")
                        u = off + i
                        hi = zc[:, bass.ds(u, 1), 0, :].rearrange("p o k -> p (o k)")
                        lo = zc[:, bass.ds(u, 1), 1, :].rearrange("p o k -> p (o k)")
                        dve.tensor_scalar(row[:, 0:127], row[:, 0:127], mv[:, bass.ds(i, 1), 0], rs[:, bass.ds(i, 1)],
                                          ALU.subtract, ALU.mult).then_inc(s["z_full"], 1)
                        dve.wait_ge(s["z_full"], u + 1)
                        dve.tensor_copy(hi, row).then_inc(s["z_hi"], 1)
                        dve.wait_ge(s["z_hi"], u + 1)
                        dve.tensor_tensor(lo, row, hi, ALU.subtract).then_inc(s["z_ready"], 1)
                    dve.wait_ge(s["z_ready"], off + n)
                    dve.sem_inc(s["slab_free"], 1)

            with dve.Fori(0, B) as b:
                n, off = load_counts(dve, b)
                base = off + 2 * b
                for half in range(2):
                    dve.wait_ge(s["q_scores"], 2 * base + half + 1)
                    dve.tensor_copy(mrun[:, half * GC:half * GC + GC],
                                    ps[:, 1 + 2 * half:3 + 2 * half, :].rearrange("p k n -> p (k n)")
                                    ).then_inc(s["q_max"], 1)
                with dve.Fori(0, n) as i:
                    u = base + i + 1
                    for half in range(2):
                        m = mrun[:, half * GC:half * GC + GC]
                        dve.wait_ge(s["q_scores"], 2 * u + half + 1)
                        dve.wait_ge(s["q_max"], 2 * u + half + 1)
                        dve.scalar_tensor_tensor(out=m, in0=ps[:, 1 + 2 * half:3 + 2 * half, :]
                                                 .rearrange("p k n -> p (k n)"),
                                                 scalar=mbias[:, bass.ds(NC * b + NC - 1 - i, 1)], in1=m,
                                                 op0=ALU.add, op1=ALU.max).then_inc(s["q_max"], 1)
                u = base + n + 1
                for half in range(2):
                    dve.wait_ge(s["q_scores"], 2 * u + half + 1)
                    dve.tensor_reduce(mall[:, half * HG:half * HG + HG],
                                      ps[:, 1 + 2 * half:3 + 2 * half, :].rearrange("p k (h n) -> p (k h) n", n=128),
                                      AX_X, ALU.max).then_inc(s["q_max"], 1)
                dve.wait_ge(s["q_max"], 2 * u + 4)
                dve.tensor_tensor(r32[:], c32[:, bass.ds(b, 1), :, :].rearrange("p o t h -> p (o t) h"),
                                  mall[:, None, :].broadcast_to([128, 2, H]), ALU.subtract).then_inc(s["r_seq"], 1)
                dve.wait_ge(s["r_seq"], 2 * b + 1)
                dve.wait_ge(s["rT_done"], b + 1)
                dve.tensor_scalar(rhl[:, 0, :, :], r32[:], SHIFT / XSCALE, None, ALU.add).then_inc(s["r_seq"], 1)
                dve.wait_ge(s["r_seq"], 2 * b + 2)
                dve.scalar_tensor_tensor(out=rhl[:, 1, :, :], in0=r32[:], scalar=SHIFT / XSCALE, in1=rhl[:, 0, :, :],
                                         op0=ALU.add, op1=ALU.subtract).then_inc(s["r_ready"], 1)

            with dve.Fori(0, B) as b:
                n, off = load_counts(dve, b)
                for g in range(2):
                    base = 2 * (off + b) + g * (n + 1)

                    def split(u):
                        for k in range(2):
                            dve.wait_ge(s["exp_done"], 2 * u + k + 3)
                            dve.wait_ge(s["pv_done"], 2 * u + k + 1)
                            dve.tensor_copy(ph[:, k, :], p32[:, k, :]).then_inc(s["p_hi"], 1)
                            dve.wait_ge(s["p_hi"], 2 * u + k + 1)
                            dve.tensor_tensor(pl[:, k, :], p32[:, k, :], ph[:, k, :], ALU.subtract
                                              ).then_inc(s["p_ready"], 1)

                    def sums(t, count):
                        dve.wait_ge(s["t_hi"], 2 * (2 * b + g) + count)
                        dve.scalar_tensor_tensor(out=tl[:, t, :],
                                                 in0=ps[:, 2 + 2 * t:4 + 2 * t, :].rearrange("p k n -> p (k n)"),
                                                 scalar=TSCALE, in1=th[:, t, :], op0=ALU.mult, op1=ALU.subtract
                                                 ).then_inc(s["t_lo"], 1)

                    split(base)
                    split(base + 1)
                    sums(1, 1)
                    with dve.Fori(1, n) as i:
                        split(base + i + 1)
                    sums(0, 2)
                    dve.wait_ge(s["u_done"], 2 * b + g + 2)
                    uv = ps[:, 6:8, 0:4 * (DH + 1)].rearrange("p k (h d) -> p k h d", h=4)
                    dve.reciprocal(rinv[:].rearrange("p (k h) -> p k h", k=2), uv[:, :, :, DH]).then_inc(s["u_inv"], 1)
                    dve.wait_ge(s["u_inv"], 2 * b + g + 1)
                    dve.wait_ge(s["oT_fill"], 2 * b + g + 1)
                    for k in range(2):
                        ins = dve.tensor_tensor(on[:, 4 * k:4 * k + 4, :], uv[:, k, :, 0:DH],
                                                rinv[:, 4 * k:4 * k + 4, None].broadcast_to([128, 4, DH]), ALU.mult)
                    ins.then_inc(s["on_ready"], 1)
                dve.wait_ge(s["xo_done"], b + 2)
                row = xs[:, bass.ds(b, 1), :].rearrange("p o d -> p (o d)")
                dve.tensor_tensor(row, ps[:, 7, 0:128], row, ALU.add).then_inc(s["x1_done"], 1)

            dve.wait_ge(s["x1_done"], B + 1)
            norm(xs, 2).then_inc(s["lat_ready"], 1)
            dve.wait_ge(s["lat_ready"], 2)
            dve.wait_ge(s["late_in"], LATE)
            dve.wait_ge(s["const_done"], N_CONST)
            link(dve.tensor_tensor(xs[:], xs[:], abr[:, 1:2, :].broadcast_to([128, B, D]), ALU.add))
            dve.wait_ge(s["a_fill"], 1)
            dve.tensor_scalar(qTa, ps[:, 1, :], ab[:, 0:1], None, ALU.add)
            dve.tensor_tensor(va[:, :, :, 0:DK], ps[:, 3, :].rearrange("p (b h d) -> p b h d", b=B, h=AH)
                              if False else ps[:, 3, :].rearrange("p (b h d) -> p b h d", b=B, h=AH),
                              abr[:, 0, :].rearrange("p (h d) -> p h d", h=AH)[:, None, :, :]
                              .broadcast_to([128, B, AH, DK]), ALU.add)
            dve.memset(va[:, :, :, DK:DK + 1], 1.0)
            link(dve.tensor_scalar(kTa, ps[:, 2, :], ab[:, 1:2], None, ALU.add))
            for b in range(B):
                ins = dve.tensor_tensor(kblk[:, b, :, :],
                                        kTa[:, None, b * 128:b * 128 + 128].broadcast_to([128, 4, 128]),
                                        headmask[:, :, None].broadcast_to([128, 4, 128]), ALU.mult)
            ins.then_inc(s["a_done"], 1)
            for b in range(B):
                dve.wait_ge(s["a_s"], b + 1)
                link(dve.tensor_reduce(amax[:, b, :], ps[:, 0:4, :].rearrange("p g (h k) -> p (g h) k", h=4),
                                       AX_X, ALU.max))
                dve.tensor_scalar(nmax[:, b, :], amax[:, b, :], -ASCALE, None, ALU.mult).then_inc(s["a_max"], 1)
                for g in range(2):
                    dve.wait_ge(s["a_tr"], 2 * b + g + 1)
                    if b >= 1:
                        dve.wait_ge(s["a_pv"], b)
                    dve.tensor_copy(paT[:, 8 * g:8 * g + 8, :].rearrange("p h k -> p (h k)"),
                                    ps[:, 4:6, :].rearrange("p g n -> p (g n)")).then_inc(s["a_trc"], 1)
                dve.wait_ge(s["a_pv"], b + 1)
                o = ps[:, 6, 0:9 * AH].rearrange("p (h d) -> p h d", h=AH)
                link(dve.reciprocal(ra, o[:, :, DK]))
                if b >= 1:
                    dve.wait_ge(s["a_oT"], b)
                dve.tensor_tensor(oa.rearrange("p (h d) -> p h d", h=AH), o[:, :, 0:DK],
                                  ra[:, :, None].broadcast_to([128, AH, DK]), ALU.mult).then_inc(s["a_o"], 1)
                dve.wait_ge(s["a_y"], b + 1)
                dve.tensor_tensor(xs[:, b, :], ps[:, 7, 128:256], xs[:, b, :], ALU.add).then_inc(s["a_x2"], 1)

            dve.wait_ge(s["a_x2"], B)
            norm(xs, 3).then_inc(s["lat_ready"], 1)
            dve.wait_ge(s["lat_ready"], 3)
            dve.wait_ge(s["r_log"], 1)
            logits = ps[:, 1, 0:B * E].rearrange("p (b e) -> p b e", b=B)
            link(dve.tensor_reduce(lgm, logits, AX_X, ALU.max))
            dve.tensor_tensor(lg, logits, lgm[:, :, None].broadcast_to([128, B, E]), ALU.subtract
                              ).then_inc(s["r_log"], 1)
            dve.wait_ge(s["r_log"], 2)
            other = lg[:, :, None, :].broadcast_to([128, B, E, E])
            own = lg[:, :, :, None].broadcast_to([128, B, E, E])
            g4 = gtm.rearrange("p (b e) f -> p b e f", b=B)
            e4 = eqm.rearrange("p (b e) f -> p b e f", b=B)
            dve.tensor_tensor(g4, other, own, ALU.is_gt)
            link(dve.tensor_tensor(e4, other, own, ALU.is_equal))
            link(dve.tensor_tensor(e4, e4, tri[:, None, :, :].broadcast_to([128, B, E, E]), ALU.mult))
            link(dve.tensor_tensor(gtm, gtm, eqm, ALU.add))
            dve.tensor_reduce(rank, gtm, AX_X, ALU.add)
            dve.wait_ge(s["r_exp"], 1)
            link(dve.tensor_reduce(sm, ex, AX_X, ALU.add))
            dve.reciprocal(sm, sm)
            link(dve.scalar_tensor_tensor(out=pr[:].rearrange("p b e -> p (b e)"), in0=rank, scalar=1.5,
                                          in1=ex[:].rearrange("p b e -> p (b e)"), op0=ALU.is_lt, op1=ALU.mult))
            link(dve.scalar_tensor_tensor(out=pr, in0=pr, scalar=0.5, in1=sm[:, :, None].broadcast_to([128, B, E]),
                                          op0=ALU.mult, op1=ALU.mult))
            for c in range(2 * E):
                bank = 2 + 2 * (c % 2)
                dve.wait_ge(s["f_t"], c + 1)
                if c >= 2:
                    dve.wait_ge(s["f_g"], c - 1)
                link(dve.scalar_tensor_tensor(out=gg[:, c % 2, :], in0=tt[:, c % 2, :], scalar=1.0, in1=ps[0:FH, bank, :],
                                              op0=ALU.add, op1=ALU.mult))
                dve.tensor_tensor(gT[0:FH, c, :], gg[:, c % 2, :], ps[0:FH, bank + 1, :], ALU.mult).then_inc(s["f_g"], 1)
            for b in range(B):
                for e in range(E):
                    if e % 4 == 0:
                        dve.wait_ge(s["f_o"], 2 * b + e // 4 + 1)
                    ins = dve.scalar_tensor_tensor(out=xs[:, b, :], in0=ps[:, 6 + e // 4, (e % 4) * 128:(e % 4) * 128 + 128],
                                                   scalar=pr[:, b, e:e + 1], in1=xs[:, b, :],
                                                   op0=ALU.mult, op1=ALU.add)
                    if e % 4 == 3:
                        ins.then_inc(s["f_acc"], 1)
                        dve.wait_ge(s["f_acc"], 2 * b + e // 4 + 1)
                    else:
                        link(ins)
            dve.sem_inc(s["ready_out"], 1)


_INS = ["x", "ctx_1024", "mask_BxS2_bk0", "L0_xattn_g1", "L0_xattn_b1", "L0_xattn_g2", "L0_xattn_b2",
        "L0_xattn_Wq", "L0_xattn_Wkv", "L0_xattn_Wout", "L0_attn_Wq", "L0_attn_bq", "L0_attn_Wk",
        "L0_attn_bk", "L0_attn_Wv", "L0_attn_bv", "L0_attn_Wo", "L0_attn_bo", "L0_ffn_router_weight",
        "L0_ffn_w1", "L0_ffn_w2"]


def kernel(**inputs):
    import numpy as _np
    import concourse.bacc as _bacc
    from concourse import mybir as _mybir
    from concourse.bass_utils import run_bass_kernel_spmd as _run

    nc = _bacc.Bacc("TRN2", target_bir_lowering=False, num_devices=1)
    arrays, args = {}, []
    for name in _INS:
        a = _np.ascontiguousarray(inputs[name])
        arrays[f"in_{name}"] = a
        args.append(nc.dram_tensor(f"in_{name}", a.shape, _mybir.dt.from_np(a.dtype), kind="ExternalInput").ap())
    args.append(nc.dram_tensor("out_x", (4, 128, 128), F32, kind="ExternalOutput").ap())
    perceiver_block(nc, *args)
    r = _run(nc, [arrays], core_ids=[0])
    return r.results[0]["out_x"]
```

```python
from contextlib import ExitStack

import concourse.bass as bass
from concourse import mybir

ALU = mybir.AluOpType
ACT = mybir.ActivationFunctionType
AX_X = mybir.AxisListType.X
F32 = mybir.dt.float32
F16 = mybir.dt.float16
BF16 = mybir.dt.bfloat16
I32 = mybir.dt.int32
U8 = mybir.dt.uint8

EPS = 1e-5
MASKED = -1e30
OUTSIDE = -3e9
WINDOW = 32


def perceiver_block(nc, x, ctxt, mask, g1, b1, g2, b2, Wq, Wkv, Wout,
                    aWq, abq, aWk, abk, aWv, abv, aWo, abo, rw, w1, w2, out):
    B, L, D = x.shape
    S = ctxt.shape[1]
    INNER = Wq.shape[1]
    DH = 64
    H = INNER // DH
    NC = S // 128
    NJ = INNER // 128
    HG = H // 2
    GC = HG * L
    QB = H * L
    E, _, F2 = w1.shape
    F = F2 // 2
    FH = F // 2
    AH = 16
    DK = D // AH
    ASCALE = DK ** -0.5
    XSCALE = 1.0 / 8.0
    SHIFT = 4.0
    TSCALE = 2.0 ** -5
    BL = B * L

    with ExitStack() as ctx:
        def sb(name, shape, dt):
            return ctx.enter_context(nc.sbuf_tensor(name, shape, dt))

        def sem(name):
            return ctx.enter_context(nc.semaphore(name))

        ps = ctx.enter_context(nc.psum_tensor("ps", [128, 8, 512], F32))

        ident = sb("ident", [128, 128], F32)
        identh = sb("identh", [128, 128], F16)
        identb = sb("identb", [128, 128], BF16)
        fold = sb("fold", [128, 128], F32)
        gt = sb("gt", [128, 2, 128], F32)
        gb = sb("gb", [128, 4], F32)
        zero2 = sb("zero2", [128, 130], F16)
        neghalf = sb("neghalf", [128, 64], F32)
        weight = sb("weight", [1, 64], F32)
        band = sb("band", [128, 128], BF16)
        headmask = sb("headmask", [128, 4], F32)
        tri = sb("tri", [128, 8, 8], F32)
        mk = sb("mk", [B * NC, 128], U8)
        mkf = sb("mkf", [B * NC, 128], F32)
        flag = sb("flag", [B * NC, 1], F32)
        lastc = sb("lastc", [1, 64], F32)
        metaf = sb("metaf", [1, 12], F32)
        place = sb("place", [1, 3, B], F32)
        packf = sb("packf", [1, 3], F32)
        pack = sb("pack", [1, 3], I32)
        mbias = sb("mbias", [128, B * NC], F32)
        xs = sb("xs", [128, B, D], F32)
        xn = sb("xn", [128, B, D], F32)
        st = sb("st", [128, 2, NC, 6], F32)
        mv = sb("mv", [128, 2, NC, 2], F32)
        rs = sb("rs", [128, 2, NC], F32)
        stl = sb("stl", [128, B, 6], F32)
        mvl = sb("mvl", [128, B, 2], F32)
        rsl = sb("rsl", [128, B], F32)
        zl = sb("zl", [128, B, 2, 128], F16)
        zlT = sb("zlT", [128, 2, B, 128], F16)
        zc = sb("zc", [128, B * NC, 2, 128], F16)
        zcT = sb("zcT", [128, B * NC, 2, 128], F16)
        raw = sb("raw", [128, 2, NC, 128], F32)
        qq = sb("qq", [128, 2, 2, B, QB], F16)
        reg = sb("reg", [128, 9216], F32)
        wq_s = reg[:, 0:1024]
        wkv_s = reg[:, 1024:3072]
        wkT = [reg[:, 3072 + 1024 * k:4096 + 1024 * k].bitcast(F16)
               .rearrange("p (j t a) -> p j t a", j=NJ, t=2) for k in range(2)]
        qT = [reg[:, 5120 + 2048 * k:7168 + 2048 * k].bitcast(F16)
              .rearrange("p (j n) -> p j n", j=NJ) for k in range(2)]
        wqt = zc[:].rearrange("p u a k -> p (u a k)")[:, 0:2 * INNER].rearrange("p (a n) -> p a n", a=2)
        p32 = reg[:, 0:1024].rearrange("p (j n) -> p j n", j=2)
        ph = reg[:, 1024:1536].bitcast(F16).rearrange("p (j n) -> p j n", j=2)
        pl = reg[:, 1536:2048].bitcast(F16).rearrange("p (j n) -> p j n", j=2)
        th = reg[:, 2048:3072].bitcast(F16).rearrange("p (t n) -> p t n", t=2)
        tl = reg[:, 3072:4096].bitcast(F16).rearrange("p (t n) -> p t n", t=2)
        on = reg[:, 4096:4608].rearrange("p (h d) -> p h d", h=HG)
        oT = reg[:, 4608:5632].rearrange("p (j n) -> p j n", j=NJ)
        mrun = reg[:, 7168:9216]
        rinv = sb("rinv", [128, HG], F32)
        wv = sb("wv", [128, 2, 2, H, DH + 1], F16)
        cm = sb("cm", [128, 2, NJ, 2, 2], F16)
        wo_s = sb("wo_s", [128, NJ, D], F32)
        c32 = sb("c32", [128, B, 2, H], F32)
        mall = sb("mall", [128, H], F32)
        r32 = sb("r32", [128, 2, H], F32)
        rhl = sb("rhl", [128, 2, 2, H], F16)
        rT = sb("rT", [64, 128], F16)
        rawflat = raw[:].rearrange("p s c k -> p (s c k)")
        w1_s = rawflat[:, 0:E * F2].rearrange("p (e f) -> p e f", e=E)
        aw = rawflat[:, 2816:3328].rearrange("p (k n) -> p k n", k=4)
        abr = rawflat[:, 3328:3584].rearrange("p (k n) -> p k n", k=2)
        rw_s = rawflat[:, 3584:3592]
        ab = rawflat[:, 3592:3594]
        late = qq[:].rearrange("p a t b n -> p (a t b n)").bitcast(F32)
        xT = late[:, 0:512]
        qTa = late[:, 512:1024]
        kTa = late[:, 1024:1536]
        kblk = late[:, 1536:3584].rearrange("p (b h k) -> p b h k", b=B, h=4)
        va = late[:, 3584:4160].rearrange("p (b h d) -> p b h d", b=B, h=AH)
        amax = late[:, 4160:4224].rearrange("p (b h) -> p b h", b=B)
        nmax = late[:, 4224:4288].rearrange("p (b h) -> p b h", b=B)
        pa = late[:, 4288:6336].rearrange("p (h k) -> p h k", h=AH)
        paT = late[:, 6336:8384].rearrange("p (h k) -> p h k", h=AH)
        ra = late[:, 8384:8400]
        oa = late[:, 8400:8528]
        oaT = late[:, 8528:8656]
        lg = late[:, 8656:8688].rearrange("p (b e) -> p b e", b=B)
        lgm = late[:, 8688:8692]
        ex = late[:, 8692:8724].rearrange("p (b e) -> p b e", b=B)
        sm = late[:, 8724:8728]
        gtm = late[:, 8728:8984].rearrange("p (b f) -> p b f", f=E)
        eqm = late[:, 8984:9240].rearrange("p (b f) -> p b f", f=E)
        rank = late[:, 9240:9272]
        pr = late[:, 9272:9304].rearrange("p (b e) -> p b e", b=B)
        tt = late[0:FH, 9304:10328].rearrange("p (k n) -> p k n", k=2)
        gg = late[0:FH, 10328:11352].rearrange("p (k n) -> p k n", k=2)
        w2_s = reg[0:FH, 7168:9216].rearrange("p (c d) -> p c d", c=2 * E)
        w1p = [zcT[:].rearrange("p u a k -> p (u a k)")[:, k * E * F2:(k + 1) * E * F2]
               .rearrange("p (e f) -> p e f", e=E) for k in range(2)]
        xTp = [late[:, 11352 + 256 * k:11608 + 256 * k].bitcast(F16) for k in range(2)]
        gT = zc[:].rearrange("p u a k -> p (u a k)").bitcast(F32)[:, 0:8192].rearrange(
            "p (c n) -> p c n", c=2 * E)

        names = """mask_in x_in gb_in wk_in wv_in wq_in w_split f_w wo_in late_in ctx_in0 ctx_in1 const_done
            pool_fold fl_done cnt_done meta_done mb_done seq gt_done stat_ready rs_ready
            lat_ready latT_done fill hi lo c_done c_used ctx_stat ctx_rs z_ready zT_fill zT_copied
            slab_free q_scores q_max r_ready rT_done rT_copied row_set
            sc_ready exp_done p_ready pv_done t_ready t_hi t_lo u_done on_ready oT_fill oT_copied
            xo_done x1_done
            xT_fill xT_done ctx_bn ctx_ag z_full z_hi r_seq p_hi u_inv passed_dve passed_sp passed_pe passed_act a_fill a_done a_s a_max a_exp a_tr a_trc a_pv a_o a_oT a_oTc a_y a_x2
            r_log r_exp f_y f_t f_g f_o f_acc out_sent ready_out pre""".split()
        s = {n: sem(n) for n in names}

        mask_rows = mask.rearrange("b (c k) -> (b c) k", c=NC)
        x_rows = x.rearrange("b l d -> l b d")
        out_rows = out.rearrange("b l d -> l b d")
        ctx_rows = ctxt.rearrange("b (c k) d -> b c k d", c=NC)

        T_WK, T_WQ, T_WV, T_LT, T_QT, T_QQ = 0, 2, 3, 5, 6, 10
        N_FILL = T_QQ + H
        block = ctx.enter_context(nc.Block())

        def counts(eng):
            n = eng.value_load(pack[0:1, 0:1], min_val=0, max_val=2 ** 24)
            off = eng.value_load(pack[0:1, 1:2], min_val=0, max_val=2 ** 24)
            return (lambda b: nc.s_assert_within(eng.snap((n >> (b * 6)) & 63), 2, NC, skip_runtime_bounds_check_because="clamped when packed"),
                    lambda b: nc.s_assert_within(eng.snap((off >> (b * 6)) & 63), 0, 3 * NC, skip_runtime_bounds_check_because="clamped when packed"))

        def prepared(e, part):
            src = ps[:, 2 * (e % 4):2 * (e % 4) + 2, :]
            flat = src.rearrange("p k n -> p (k n)")
            if e < T_WQ:
                return wkT[part][:, 4 * e:4 * e + 4, :, :].rearrange("p j t a -> p (j t a)"), flat
            if e < T_WV:
                return wqt[:, part, :], flat
            if e < T_LT:
                return wv[:, part, e - T_WV, :, 0:DH], src.rearrange("p k (h d) -> p (k h) d", h=8)
            if e < T_QT:
                return zlT[:].rearrange("p a b l -> p (a b l)"), src[:, 0, :].bitcast(F16)
            if e < T_QQ:
                k = 2 * (e - T_QT)
                return qT[part][:, k:k + 2, :].rearrange("p j n -> p (j n)"), flat
            h = e - T_QQ
            return (qq[:, part, :, :, h * 128:h * 128 + 128],
                    src.rearrange("p t (b l) -> p t b l", b=B))

        @block.sync
        def _(sp):
            sp.dma_start(mk[:], mask_rows).then_inc(s["mask_in"], 16)
            sp.dma_start(xs[:], x_rows).then_inc(s["x_in"], 16)
            sp.dma_start(wkv_s[:, 0:INNER], Wkv[:, 0:INNER]).then_inc(s["wk_in"], 16)
            sp.dma_start(wq_s, Wq).then_inc(s["wq_in"], 16)
            sp.dma_start(wkv_s[:, INNER:], Wkv[:, INNER:]).then_inc(s["wv_in"], 16)
            sp.dma_start(wo_s[:], Wout.rearrange("(j p) d -> p j d", p=128)).then_inc(s["wo_in"], 16)
            sp.wait_ge(s["meta_done"], 1)
            number, _ = counts(sp)
            with sp.Fori(0, B // 2) as pair:
                for par in range(2):
                    b = 2 * pair + par
                    n = number(b)
                    sp.wait_ge(s["slab_free"], b + 1)
                    sp.sem_inc(s["passed_sp"], 1)
                    with sp.Fori(0, n) as i:
                        sp.dma_start(raw[:, par, bass.ds(i, 1), :].rearrange("p o d -> p (o d)"),
                                     ctx_rows[bass.ds(b, 1), bass.ds(NC - 1 - i, 1), :, :]
                                     .rearrange("a c k d -> (a c k) d")).then_inc(s[f"ctx_in{par}"], 16)
            sp.wait_ge(s["slab_free"], B + 2)
            sp.dma_start(w1_s, w1.rearrange("e h f -> h e f")).then_inc(s["late_in"], 16)
            sp.wait_ge(s["r_ready"], B)
            sp.dma_start(w2_s, w2.rearrange("e (c f) d -> f (e c) d", c=2)).then_inc(s["late_in"], 16)
            sp.dma_start(rw_s, rw).then_inc(s["late_in"], 16)
            for k, w in enumerate((aWq, aWk, aWv, aWo)):
                sp.dma_start(aw[:, k, :], w).then_inc(s["late_in"], 16)
            for k, v in enumerate((abq, abk)):
                sp.dma_start(ab[:, k:k + 1], v.rearrange("(p o) -> p o", o=1)).then_inc(s["late_in"], 16)
            for k, v in enumerate((abv, abo)):
                sp.dma_start(abr[:, k, :], v.rearrange("(o d) -> o d", o=1).broadcast_to([128, 128])
                             ).then_inc(s["late_in"], 16)
            sp.wait_ge(s["ready_out"], 1)
            sp.dma_start(out_rows, xs[:]).then_inc(s["out_sent"], 16)
            sp.wait_ge(s["out_sent"], 16)
        LATE = 16 * 11

        @block.gpsimd
        def _(pool):
            order = [0]

            def link(ins):
                order[0] += 1
                ins.then_inc(s["const_done"], 1)
                pool.wait_ge(s["const_done"], order[0])

            link(pool.memset(ident[:], 0.0))
            link(pool.affine_select(out=ident[:], in_=ident[:], compare_op=ALU.not_equal, fill=1.0,
                                    base=0, pattern=[[-1, 128]], channel_multiplier=1))
            link(pool.iota(weight[:].rearrange("p (b c) -> p b c", b=B), [[0, B], [-1, NC]], base=NC,
                           channel_multiplier=0, allow_small_or_imprecise_dtypes=True))
            link(pool.affine_select(out=fold[:], in_=ident[:], compare_op=ALU.not_equal, fill=-1.0,
                                    base=-127, pattern=[[0, 128]], channel_multiplier=1))
            link(pool.tensor_copy(identh[:], ident[:]))
            link(pool.memset(neghalf[:], -0.5))
            pool.memset(zero2[:], 0.0).then_inc(s["pool_fold"], 1)
            for k in range(2):
                pool.wait_ge(s["stat_ready"], k + 1)
                pool.tensor_tensor(rsl[:], rsl[:], neghalf[:, 0:B], ALU.pow).then_inc(s["rs_ready"], 1)
            pool.memset(wv[:], 0.0).then_inc(s["pool_fold"], 1)
            pool.wait_ge(s["pool_fold"], 2)
            for t in range(2):
                pool.affine_select(out=wv[:, 0, t, :, DH], in_=wv[:, 0, t, :, DH],
                                   compare_op=ALU.not_equal, fill=1.0, base=-127, pattern=[[0, H]],
                                   channel_multiplier=1).then_inc(s["pool_fold"], 1)
            for b in range(B):
                pool.wait_ge(s["ctx_stat"], b + 1)
                pool.tensor_tensor(rs[:, b % 2, :], rs[:, b % 2, :], neghalf[:, 0:NC], ALU.pow).then_inc(s["ctx_rs"], 1)
            link(pool.memset(band[:], 0.0))
            link(pool.affine_select(out=band[:], in_=band[:], compare_op=ALU.is_ge, fill=OUTSIDE,
                                    base=WINDOW // 2, pattern=[[-1, 128]], channel_multiplier=1))
            link(pool.affine_select(out=band[:], in_=band[:], compare_op=ALU.is_ge, fill=OUTSIDE,
                                    base=WINDOW // 2, pattern=[[1, 128]], channel_multiplier=-1))
            link(pool.tensor_copy(identb[:], ident[:]))
            link(pool.memset(headmask[:], 0.0))
            for g in range(4):
                sub = headmask[32 * g:32 * g + 32, :]
                link(pool.memset(sub, 1.0))
                link(pool.affine_select(out=sub, in_=sub, compare_op=ALU.is_ge, fill=0.0, base=0,
                                        pattern=[[-DK, 4]], channel_multiplier=1))
                link(pool.affine_select(out=sub, in_=sub, compare_op=ALU.is_ge, fill=0.0, base=DK - 1,
                                        pattern=[[DK, 4]], channel_multiplier=-1))
            link(pool.memset(tri[:], 1.0))
            link(pool.affine_select(out=tri[:], in_=tri[:], compare_op=ALU.is_gt, fill=0.0, base=0,
                                    pattern=[[1, E], [-1, E]], channel_multiplier=0))
            for k in range(2):
                pool.wait_ge(s["stat_ready"], k + 3)
                pool.tensor_tensor(rsl[:], rsl[:], neghalf[:, 0:B], ALU.pow).then_inc(s["rs_ready"], 1)
                if k == 0:
                    pool.wait_ge(s["late_in"], LATE)
                    for e in range(E):
                        pool.tensor_copy(w1p[0][:, e, :], w1_s[:, e, :]).then_inc(s["w_split"], 1)
                        pool.wait_ge(s["w_split"], 2 * e + 1)
                        pool.tensor_tensor(w1p[1][:, e, :], w1_s[:, e, :], w1p[0][:, e, :], ALU.subtract
                                           ).then_inc(s["w_split"], 1)
        N_CONST = 6 + 5 + 12 + 2

        @block.tensor
        def _(pe):
            def half(e, k):
                return ps[:, 2 * (e % 4) + k, :]

            pe.wait_ge(s["const_done"], 5)
            pe.wait_ge(s["fl_done"], 2)
            pe.matmul(ps[0:1, 6, 0:64], flag[:], ident[0:64, 0:64], start=True, stop=True)
            pe.transpose(ps[:, 7, 0:64], mkf[:], ident[0:64, 0:64]).then_inc(s["cnt_done"], 1)
            pe.wait_ge(s["gt_done"], 1)
            pe.wait_ge(s["wk_in"], 16)
            for j in range(NJ):
                e = T_WK + j // 4
                mm = pe.matmul(half(e, j // 2 % 2)[:, j % 2 * 256:j % 2 * 256 + 256], wkv_s[:, j * 128:j * 128 + 128],
                               gt[:].rearrange("p t a -> p (t a)"), start=True, stop=True)
                if j % 4 == 3:
                    mm.then_inc(s["fill"], 1)
            pe.wait_ge(s["wq_in"], 16)
            for k in range(2):
                mm = pe.matmul(half(T_WQ, k), gt[:, 1, :], wq_s[:, k * 512:k * 512 + 512], start=True, stop=True)
            mm.then_inc(s["fill"], 1)
            pe.wait_ge(s["wv_in"], 16)
            pe.wait_ge(s["meta_done"], 1)
            pe.wait_ge(s["mb_done"], 1)
            for t in range(2):
                e = T_WV + t
                if e >= 4:
                    pe.wait_ge(s["lo"], e - 3)
                for k in range(2):
                    mm = pe.matmul(half(e, k), gt[:, t, :], wkv_s[:, INNER + k * 512:INNER + k * 512 + 512],
                                   start=True, stop=True)
                mm.then_inc(s["fill"], 1)
            pe.wait_ge(s["lat_ready"], 1)
            pe.wait_ge(s["lo"], T_LT - 3)
            for hl in range(2):
                for b in range(B):
                    c = (hl * B + b) * 128
                    mm = pe.transpose(half(T_LT, 0).bitcast(F16)[:, c:c + 128], zl[:, b, hl, :], identh[:])
            mm.then_inc(s["fill"], 1)

            def three(dst, ah, al, bh, bl):
                pe.matmul(dst, ah, bh, start=True, stop=False)
                pe.matmul(dst, ah, bl, start=False, stop=False)
                return pe.matmul(dst, al, bh, start=False, stop=True)

            latT = [zlT[:, k, :, :].rearrange("p b l -> p (b l)") for k in range(2)]
            pe.wait_ge(s["lo"], T_LT + 1)
            for j in range(NJ):
                e = T_QT + j // 2
                w = [wqt[:, k, j * 128:j * 128 + 128] for k in range(2)]
                mm = three(half(e, j % 2), w[0], w[1], latT[0], latT[1])
                if j % 2 == 1:
                    mm.then_inc(s["fill"], 1)
            for h in range(H):
                j, r = h // 2, 64 * (h % 2)
                e = T_QQ + h
                pe.wait_ge(s["lo"], max(e - 3, T_QT + j // 2 + 1))
                for t in range(2):
                    w = [wkT[k][r:r + 64, j, t, :] for k in range(2)]
                    q = [qT[k][r:r + 64, j, :] for k in range(2)]
                    mm = three(half(e, t), w[0], w[1], q[0], q[1])
                mm.then_inc(s["fill"], 1)
            pe.wait_ge(s["lo"], N_FILL)
            pe.wait_ge(s["c_used"], 4)
            for b in range(B):
                for j in range(NJ):
                    for k in range(3):
                        lhs = qT[1 if k == 1 else 0][:, j, b * 128:b * 128 + 128]
                        mm = pe.matmul(ps[:, 0, b * 32 + 4 * j:b * 32 + 4 * j + 4], lhs,
                                       cm[:, 1 if k == 2 else 0, j, :, :].rearrange("p t r -> p (t r)"), start=(k == 0), stop=(k == 2))
            mm.then_inc(s["c_done"], 1)

            number, before = counts(pe)
            with pe.Fori(0, B) as b:
                n, off = number(b), before(b)
                with pe.Fori(0, n) as i:
                    u = off + i
                    pe.wait_ge(s["z_ready"], u + 1)
                    pe.wait_ge(s["zT_copied"], u + 1)
                    for hl in range(2):
                        mm = pe.transpose(ps[:, 5, :].bitcast(F16)[:, hl * 128:hl * 128 + 128],
                                          zc[:, bass.ds(u, 1), hl, :].rearrange("p o d -> p (o d)"), identh[:])
                    mm.then_inc(s["zT_fill"], 1)

            with pe.Fori(0, B) as b:
                n, off = number(b), before(b)
                base = off + 2 * b

                def fast(zT, t, u):
                    for half in range(2):
                        pe.wait_ge(s["q_max"], 2 * u + half + 1)
                        for k in range(2):
                            c = (2 * half + k) * 512
                            mm = pe.matmul(ps[:, 1 + 2 * half + k, :], zT,
                                           qq[:, 0, t, bass.ds(b, 1), c:c + 512].rearrange("p o n -> p (o n)"),
                                           start=True, stop=True)
                        mm.then_inc(s["q_scores"], 1)

                fast(zlT[:, 0, bass.ds(b, 1), :].rearrange("p o d -> p (o d)"), 1, base)
                with pe.Fori(0, n) as i:
                    pe.wait_ge(s["zT_copied"], off + i + 2)
                    fast(zcT[:, bass.ds(off + i, 1), 0, :].rearrange("p o d -> p (o d)"), 0, base + i + 1)
                for half in range(2):
                    pe.wait_ge(s["q_max"], 2 * (base + n + 1) + 2)
                    for k in range(8):
                        c = (8 * half + k) * 128
                        mm = pe.transpose(ps[:, 1 + 2 * half + k // 4, (k % 4) * 128:(k % 4) * 128 + 128],
                                          mrun[:, c:c + 128], ident[:])
                    mm.then_inc(s["q_scores"], 1)
                pe.wait_ge(s["r_ready"], b + 1)
                pe.wait_ge(s["rT_copied"], b + 1)
                pe.sem_inc(s["passed_pe"], 1)
                pe.transpose(ps[0:64, 6, :].bitcast(F16)[:, 0:128],
                             rhl[:].rearrange("p a t h -> p (a t h)"), identh[:]).then_inc(s["rT_done"], 1)

            SC, T1, T2, UB = 0, 2, 4, 6

            def at(tile, hl, idx):
                if tile is zlT:
                    return tile[:, hl, bass.ds(idx, 1), :].rearrange("p o d -> p (o d)")
                return tile[:, bass.ds(idx, 1), hl, :].rearrange("p o d -> p (o d)")

            def head_values(b, g):
                q = 2 * b + g
                pe.wait_ge(s["t_lo"], 2 * q + 4)
                pe.wait_ge(s["oT_copied"], q + 1)
                pe.wait_ge(s["x1_done"], b + 1)
                for h in range(HG):
                    o = ps[:, UB + h // 4, (h % 4) * (DH + 1):(h % 4 + 1) * (DH + 1)]
                    c = h * 128
                    step = 0
                    for t in range(2):
                        for a, w in ((th, 0), (th, 1), (tl, 0)):
                            mm = pe.matmul(o, a[:, t, c:c + 128], wv[:, w, t, g * HG + h, :],
                                           start=(step == 0), stop=(step == 5))
                            step += 1
                mm.then_inc(s["u_done"], 1)

            def turn_heads(b, g):
                pe.wait_ge(s["on_ready"], 2 * b + g + 1)
                for k in range(4):
                    mm = pe.transpose(ps[:, UB, k * 128:k * 128 + 128],
                                      on[:, 2 * k:2 * k + 2, :].rearrange("p h d -> p (h d)"), ident[:])
                mm.then_inc(s["oT_fill"], 1)

            def project(b):
                pe.wait_ge(s["oT_copied"], 2 * b + 3)
                for j in range(NJ):
                    mm = pe.matmul(ps[:, UB + 1, 0:128], oT[:, j, :], wo_s[:, j, :],
                                   start=(j == 0), stop=(j == NJ - 1))
                mm.then_inc(s["xo_done"], 1)

            def batch(b, first):
                n, off = number(b), before(b)
                pe.wait_ge(s["row_set"], 64 * b + 128)
                for g in range(2):
                    base = 2 * (off + b) + g * (n + 1)

                    def scores(zT, t, u):
                        for k in range(2):
                            pe.wait_ge(s["exp_done"], 2 * u + k + 1)
                            c = g * GC + k * 512
                            rhs = [qq[:, a, t, bass.ds(b, 1), c:c + 512].rearrange("p o n -> p (o n)")
                                   for a in range(2)]
                            three(ps[:, SC + k, :], zT[0], zT[1], rhs[0], rhs[1]).then_inc(s["sc_ready"], 1)

                    def values(z, dst, u, alone):
                        for k in range(2):
                            pe.wait_ge(s["p_ready"], 2 * u + k + 3)
                            d = ps[:, dst + k, :]
                            pe.matmul(d, z[0], ph[:, k, :], start=alone, stop=False, skip_group_check=True)
                            pe.matmul(d, z[0], pl[:, k, :], start=False, stop=False, skip_group_check=True)
                            mm = pe.matmul(d, z[1], ph[:, k, :], start=False, stop=alone, skip_group_check=True)
                            mm.then_inc(s["pv_done"], 1)

                    scores([at(zlT, 0, b), at(zlT, 1, b)], 1, base)
                    scores([at(zcT, 0, off), at(zcT, 1, off)], 0, base + 1)
                    last = (b, 0) if g == 1 else (b - 1, 1)
                    if g == 1 or not first:
                        head_values(*last)
                    pe.wait_ge(s["t_lo"], 2 * (2 * b + g) + 2)
                    values([at(zl, 0, b), at(zl, 1, b)], T2, base, True)
                    if g == 1 or not first:
                        turn_heads(*last)
                    for k in range(2):
                        pe.matmul(ps[:, T1 + k, 0:2], zero2[:, 0:128], zero2[:, 128:130],
                                  start=True, stop=False, skip_group_check=True)
                    with pe.Fori(1, n) as i:
                        scores([at(zcT, 0, off + i), at(zcT, 1, off + i)], 0, base + i + 1)
                        values([at(zc, 0, off + i - 1), at(zc, 1, off + i - 1)], T1, base + i, False)
                    if g == 0 and not first:
                        project(b - 1)
                    values([at(zc, 0, off + n - 1), at(zc, 1, off + n - 1)], T1, base + n, False)

            batch(0, True)
            with pe.Fori(1, B) as b:
                batch(b, False)
            head_values(B - 1, 1)
            turn_heads(B - 1, 1)
            project(B - 1)

            def turn_norm(k):
                pe.wait_ge(s["lat_ready"], k + 2)
                for b in range(B):
                    mm = pe.transpose(ps[:, 0, b * 128:b * 128 + 128], xn[:, b, :], ident[:])
                mm.then_inc(s["xT_fill"], 1)
                pe.wait_ge(s["xT_done"], 1 if k == 0 else 3)

            pe.wait_ge(s["late_in"], LATE)
            pe.wait_ge(s["const_done"], N_CONST)
            turn_norm(0)
            pe.matmul(ps[:, 1, :], aw[:, 0, :], xT, start=True, stop=True)
            pe.matmul(ps[:, 2, :], aw[:, 1, :], xT, start=True, stop=True)
            for b in range(B):
                mm = pe.matmul(ps[:, 3, b * 128:b * 128 + 128], xT[:, b * 128:b * 128 + 128], aw[:, 2, :],
                               start=True, stop=True)
            mm.then_inc(s["a_fill"], 1)
            pe.wait_ge(s["a_done"], 1)
            STEPS = 4 * B

            def local_scores(k):
                b, g = k // 4, k % 4
                pe.wait_ge(s["a_done"], b + 1)
                if k >= 3:
                    pe.wait_ge(s["a_exp"], k - 2)
                pe.matmul(ps[:, k % 3, :], qTa[32 * g:32 * g + 32, b * 128:b * 128 + 128],
                          kblk[32 * g:32 * g + 32, b, :, :].rearrange("p h k -> p (h k)"), start=True, stop=False)
                pe.matmul(ps[:, k % 3, :], identb[:], band[:, None, :].broadcast_to([128, 4, 128]),
                          start=False, stop=True).then_inc(s["a_s"], 1)

            def local_turn(k):
                pe.wait_ge(s["a_exp"], k + 1)
                if k >= 2:
                    pe.wait_ge(s["a_trc"], k - 1)
                for m in range(4):
                    mm = pe.transpose(ps[:, 4 + k % 2, m * 128:m * 128 + 128], pa[:, 4 * (k % 4) + m, :], ident[:])
                mm.then_inc(s["a_tr"], 1)

            def local_values(k):
                b, g = k // 4, k % 4
                pe.wait_ge(s["a_trc"], k + 1)
                if b >= 2 and g == 0:
                    pe.wait_ge(s["a_o"], b - 1)
                for m in range(4):
                    c = 9 * (4 * g + m)
                    mm = pe.matmul(ps[:, 3 + 3 * (b % 2), c:c + 9], paT[:, 4 * (k % 4) + m, :], va[:, b, 4 * g + m, :],
                                   start=True, stop=True)
                mm.then_inc(s["a_pv"], 1)

            local_scores(0)
            local_scores(1)
            for k in range(STEPS + 4):
                if k + 2 < STEPS:
                    local_scores(k + 2)
                if k < STEPS:
                    local_turn(k)
                if 1 <= k <= STEPS:
                    local_values(k - 1)
                if k % 4 == 2 and k >= 6:
                    b = (k - 6) // 4
                    pe.wait_ge(s["a_o"], b + 1)
                    if b >= 1:
                        pe.wait_ge(s["a_x2"], b)
                    pe.transpose(ps[:, 7, 0:128], oa, ident[:]).then_inc(s["a_oT"], 1)
                if k % 4 == 3 and k >= 7:
                    b = (k - 7) // 4
                    pe.wait_ge(s["a_oTc"], b + 1)
                    pe.matmul(ps[:, 7, 0:128], oaT, aw[:, 3, :], start=True, stop=True).then_inc(s["a_y"], 1)

            turn_norm(1)
            for b in range(B):
                mm = pe.matmul(ps[:, 1, b * E:b * E + E], xT[:, b * 128:b * 128 + 128], rw_s, start=True, stop=True)
            mm.then_inc(s["r_log"], 1)

            def expert_out(e):
                pe.wait_ge(s["f_g"], 2 * e + 2)
                if e >= 2:
                    pe.wait_ge(s["f_acc"], B * (e - 1))
                for b in range(B):
                    for k in range(2):
                        mm = pe.matmul(ps[:, 6 + e % 2, b * 128:b * 128 + 128],
                                       gT[0:FH, 2 * e + k, b * 128:b * 128 + 128], w2_s[:, 2 * e + k, :],
                                       start=(k == 0), stop=(k == 1))
                mm.then_inc(s["f_o"], 1)

            for e in range(E):
                pe.wait_ge(s["w_split"], 2 * e + 2)
                for c in (2 * e, 2 * e + 1):
                    if c >= 2:
                        pe.wait_ge(s["f_g"], c - 1)
                    for k in range(2):
                        f = k * F + c % 2 * FH
                        mm = three(ps[0:FH, 2 + 2 * (c % 2) + k, :], w1p[0][:, e, f:f + FH], w1p[1][:, e, f:f + FH],
                                   xTp[0], xTp[1])
                    mm.then_inc(s["f_y"], 1)
                if e >= 1:
                    expert_out(e - 1)
            expert_out(E - 1)

        @block.scalar
        def _(act):
            for k, v in enumerate((g1, b1, g2, b2)):
                act.dma_start(gb[:, k:k + 1], v.rearrange("(p o) -> p o", o=1)).then_inc(s["gb_in"], 16)
            act.sem_inc(s["zT_copied"], 1)
            act.sem_inc(s["rT_copied"], 1)
            act.sem_inc(s["row_set"], 64)
            act.sem_inc(s["exp_done"], 2)
            act.sem_inc(s["oT_copied"], 1)

            def copy(o, i):
                return act.activation(o, i, ACT.Copy)

            for e in range(N_FILL):
                act.wait_ge(s["fill"], e + 1)
                if e == T_WV:
                    act.wait_ge(s["pool_fold"], 4)
                copy(*prepared(e, 0)).then_inc(s["hi"], 1)
            act.wait_ge(s["meta_done"], 1)
            number, before = counts(act)
            with act.Fori(0, B) as b:
                n, off = number(b), before(b)
                with act.Fori(0, n) as i:
                    act.wait_ge(s["zT_fill"], off + i + 1)
                    act.sem_inc(s["passed_act"], 1)
                    copy(zcT[:, bass.ds(off + i, 1), :, :].rearrange("p o a k -> p (o a k)"),
                         ps[:, 5, :].bitcast(F16)[:, 0:256]).then_inc(s["zT_copied"], 1)
            with act.Fori(0, B) as b:
                act.wait_ge(s["rT_done"], b + 2)
                act.wait_ge(s["row_set"], 64 * b + 64)
                copy(rT[:], ps[0:64, 6, :].bitcast(F16)[:, 0:128]).then_inc(s["rT_copied"], 1)
                act.wait_ge(s["rT_copied"], b + 2)
                for k in range(4):
                    act.dma_start(qq[127:128, k // 2, k % 2, bass.ds(b, 1), :].rearrange("p o (h l) -> p (o h) l", h=H),
                                  rT[H * k:H * k + H, :]).then_inc(s["row_set"], 16)

            def batch(b, first):
                n, off = number(b), before(b)
                for g in range(2):
                    base = 2 * (off + b) + g * (n + 1)
                    q = 2 * b + g

                    def exps(u, bias):
                        for k in range(2):
                            act.wait_ge(s["sc_ready"], 2 * u + k + 1)
                            act.wait_ge(s["p_ready"], 2 * u + k + 1)
                            act.sem_inc(s["passed_act"], 1)
                            act.activation(p32[:, k, :], ps[:, k, :], ACT.Exp, bias=bias, scale=XSCALE
                                           ).then_inc(s["exp_done"], 1)

                    def sums(t, u):
                        act.wait_ge(s["pv_done"], 2 * u + 4)
                        act.activation(th[:, t, :], ps[:, 2 + 2 * t:4 + 2 * t, :].rearrange("p k n -> p (k n)"),
                                       ACT.Copy, scale=TSCALE).then_inc(s["t_hi"], 1)

                    exps(base, 0.0)
                    exps(base + 1, mbias[:, bass.ds(NC * b + NC - 1, 1)])
                    act.wait_ge(s["u_done"], q + 1)
                    sums(1, base)
                    if g == 1 or not first:
                        turned(*((b, 0) if g == 1 else (b - 1, 1)))
                    with act.Fori(1, n) as i:
                        exps(base + i + 1, mbias[:, bass.ds(NC * b + NC - 1 - i, 1)])
                    sums(0, base + n)

            def turned(b, g):
                act.wait_ge(s["oT_fill"], 2 * b + g + 2)
                act.wait_ge(s["xo_done"], b + 1)
                copy(oT[:, 4 * g:4 * g + 4, :].rearrange("p j n -> p (j n)"), ps[:, 6, :]
                     ).then_inc(s["oT_copied"], 1)

            batch(0, True)
            with act.Fori(1, B) as b:
                batch(b, False)
            turned(B - 1, 1)

            act.wait_ge(s["xT_fill"], 1)
            copy(xT, ps[:, 0, :]).then_inc(s["xT_done"], 1)
            for k in range(4 * B + 4):
                if k < 4 * B:
                    act.wait_ge(s["a_max"], k + 1)
                    if k >= 4:
                        act.wait_ge(s["a_tr"], k - 3)
                    for m in range(4):
                        h = 4 * (k % 4) + m
                        ins = act.activation(pa[:, h, :], ps[:, k % 3, m * 128:m * 128 + 128], ACT.Exp,
                                             bias=nmax[:, k // 4, h:h + 1], scale=ASCALE)
                    ins.then_inc(s["a_exp"], 1)
                if k % 4 == 2 and k >= 6:
                    b = (k - 6) // 4
                    act.wait_ge(s["a_oT"], b + 1)
                    if b >= 1:
                        act.wait_ge(s["a_y"], b)
                    copy(oaT, ps[:, 7, 0:128]).then_inc(s["a_oTc"], 1)
            act.wait_ge(s["xT_fill"], 2)
            copy(xT, ps[:, 0, :])
            copy(xTp[0], ps[:, 0, :]).then_inc(s["xT_done"], 1)
            act.wait_ge(s["r_log"], 2)
            act.activation(ex[:].rearrange("p b e -> p (b e)"), lg[:].rearrange("p b e -> p (b e)"), ACT.Exp
                           ).then_inc(s["r_exp"], 1)
            for c in range(2 * E):
                act.wait_ge(s["f_y"], c + 1)
                if c >= 2:
                    act.wait_ge(s["f_g"], c - 1)
                act.activation(tt[:, c % 2, :], ps[0:FH, 2 + 2 * (c % 2), :], ACT.Tanh, scale=0.5
                               ).then_inc(s["f_t"], 1)

        @block.vector
        def _(dve):
            dve.sem_inc(s["slab_free"], 2)
            dve.sem_inc(s["q_max"], 2)
            dve.sem_inc(s["rT_done"], 1)
            dve.sem_inc(s["p_ready"], 2)
            dve.sem_inc(s["pv_done"], 2)
            dve.sem_inc(s["t_lo"], 2)
            dve.sem_inc(s["u_done"], 1)
            dve.sem_inc(s["x1_done"], 1)
            dve.sem_inc(s["xo_done"], 1)
            dve.sem_inc(s["oT_fill"], 1)
            order = [0]

            def link(ins):
                order[0] += 1
                ins.then_inc(s["seq"], 1)
                dve.wait_ge(s["seq"], order[0])

            def norm(src, k):
                for b in range(B):
                    ins = dve.bn_stats(stl[:, b, :], src[:, b, :])
                link(ins)
                for b in range(B):
                    ins = dve.bn_aggr(mvl[:, b, :], stl[:, b, :])
                link(ins)
                dve.tensor_scalar(rsl[:], mvl[:, :, 1], EPS, None, ALU.add).then_inc(s["stat_ready"], 1)
                dve.wait_ge(s["rs_ready"], k + 1)
                for b in range(B):
                    ins = dve.tensor_scalar(xn[:, b, :], src[:, b, :], mvl[:, b, 0:1], rsl[:, b:b + 1],
                                            ALU.subtract, ALU.mult)
                return ins

            dve.memset(rs[:], 1.0)
            dve.memset(mv[:], 1.0)
            dve.memset(st[:], 1.0)
            dve.memset(metaf[:], 0.0)
            for b in range(B):
                dve.memset(place[:, :, b:b + 1], float(64 ** b))
            dve.wait_ge(s["mask_in"], 16)
            dve.tensor_copy(mkf[:], mk[:]).then_inc(s["fl_done"], 1)
            dve.wait_ge(s["fl_done"], 1)
            dve.tensor_reduce(flag[:], mkf[:], AX_X, ALU.max).then_inc(s["fl_done"], 1)
            dve.wait_ge(s["cnt_done"], 1)
            dve.tensor_scalar(mbias[:], ps[:, 7, 0:64], 1.0, -MASKED, ALU.subtract, ALU.mult).then_inc(s["mb_done"], 1)
            link(dve.tensor_tensor(lastc[:], ps[0:1, 6, 0:64], weight[:], ALU.mult))
            link(dve.tensor_reduce(metaf[:, 0:4], lastc[:].rearrange("p (b c) -> p b c", b=B), AX_X, ALU.max))
            link(dve.tensor_scalar(metaf[:, 0:4], metaf[:, 0:4], 2.0, None, ALU.max))
            dve.tensor_copy(metaf[:, 5:6], metaf[:, 0:1])
            dve.tensor_tensor(metaf[:, 6:7], metaf[:, 0:1], metaf[:, 1:2], ALU.add)
            dve.tensor_copy(metaf[:, 8:10], metaf[:, 0:2])
            link(dve.tensor_tensor(metaf[:, 10:12], metaf[:, 0:2], metaf[:, 2:4], ALU.add))
            link(dve.tensor_tensor(metaf[:, 7:8], metaf[:, 10:11], metaf[:, 1:2], ALU.add))
            link(dve.tensor_tensor(place[:], place[:], metaf[:].rearrange("p (k b) -> p k b", b=B), ALU.mult))
            link(dve.tensor_reduce(packf[:], place[:], AX_X, ALU.add))
            dve.tensor_copy(pack[:], packf[:]).then_inc(s["meta_done"], 1)

            dve.wait_ge(s["const_done"], 5)
            dve.wait_ge(s["gb_in"], 64)
            for t in range(2):
                dve.tensor_scalar(gt[:, t, 0:127], fold[:, 0:127], gb[:, 2 * t:2 * t + 1], None, ALU.mult)
                ins = dve.tensor_copy(gt[:, t, 127:128], gb[:, 2 * t + 1:2 * t + 2])
            ins.then_inc(s["gt_done"], 1)
            dve.memset(cm[:], 0.0)

            dve.wait_ge(s["x_in"], 16)
            link(norm(xs, 0))
            link(norm(xn, 1))
            link(dve.memset(xn[:, :, 127:128], 1.0))
            xnf = xn[:]
            link(dve.tensor_copy(zl[:, :, 0, :], xnf))
            dve.tensor_tensor(zl[:, :, 1, :], xnf, zl[:, :, 0, :], ALU.subtract).then_inc(s["lat_ready"], 1)

            def low(e):
                dve.wait_ge(s["hi"], e + 1)
                if e == T_LT:
                    dve.sem_inc(s["lo"], 1)
                    return
                o, i = prepared(e, 1)
                dve.tensor_tensor(o, i, prepared(e, 0)[0], ALU.subtract).then_inc(s["lo"], 1)
                if e == T_WQ - 1:
                    dve.wait_ge(s["lo"], e + 1)
                    for k in range(2):
                        for r in range(2):
                            dve.tensor_copy(cm[64 * r:64 * r + 64, k, :, :, r],
                                            wkT[k][64 * r:64 * r + 64, :, :, 127]).then_inc(s["c_used"], 1)

            number, before = counts(dve)
            loaded = dve.value_load(pack[0:1, 2:3], min_val=0, max_val=2 ** 24)

            def context_moments(b):
                par = b % 2
                n, off = number(b), before(b)
                loads = nc.s_assert_within(dve.snap((loaded >> (b * 6)) & 63), 2, 2 * NC,
                                           skip_runtime_bounds_check_because="clamped when packed")
                dve.wait_ge(s[f"ctx_in{par}"], 16 * loads)
                dve.sem_inc(s["passed_dve"], 1)
                with dve.Fori(0, n) as i:
                    dve.bn_stats(st[:, par, bass.ds(i, 1), :].rearrange("p o k -> p (o k)"),
                                 raw[:, par, bass.ds(i, 1), :].rearrange("p o k -> p (o k)")).then_inc(s["ctx_bn"], 1)
                dve.wait_ge(s["ctx_bn"], off + n)
                dve.sem_inc(s["passed_dve"], 1)
                for k in range(NC):
                    ins = dve.bn_aggr(mv[:, par, k, :], st[:, par, k, :])
                link(ins)
                dve.tensor_scalar(rs[:, par, :], mv[:, par, :, 1], EPS, None, ALU.add).then_inc(s["ctx_stat"], 1)
                link(dve.memset(raw[:, par, :, 127:128], 1.0))

            def context_rows(b):
                par = b % 2
                n, off = number(b), before(b)
                dve.wait_ge(s["ctx_rs"], b + 1)
                with dve.Fori(0, n) as i:
                    row = raw[:, par, bass.ds(i, 1), :].rearrange("p o k -> p (o k)")
                    u = off + i
                    hi = zc[:, bass.ds(u, 1), 0, :].rearrange("p o k -> p (o k)")
                    lo = zc[:, bass.ds(u, 1), 1, :].rearrange("p o k -> p (o k)")
                    dve.tensor_scalar(row[:, 0:127], row[:, 0:127], mv[:, par, bass.ds(i, 1), 0],
                                      rs[:, par, bass.ds(i, 1)], ALU.subtract, ALU.mult).then_inc(s["z_full"], 1)
                    dve.wait_ge(s["z_full"], u + 1)
                    dve.tensor_copy(hi, row).then_inc(s["z_hi"], 1)
                    dve.wait_ge(s["z_hi"], u + 1)
                    dve.tensor_tensor(lo, row, hi, ALU.subtract).then_inc(s["z_ready"], 1)
                dve.wait_ge(s["z_ready"], off + n)
                dve.sem_inc(s["slab_free"], 1)

            after = {T_QT + 3: [(context_moments, 0), (context_moments, 1)],
                     T_QQ + 3: [(context_rows, 0), (context_rows, 1)],
                     T_QQ + 8: [(context_moments, 2), (context_moments, 3)],
                     T_QQ + 12: [(context_rows, 2), (context_rows, 3)]}
            for e in range(N_FILL):
                low(e)
                for stage, b in after.get(e, []):
                    stage(b)
            dve.wait_ge(s["c_done"], 1)
            for t in range(2):
                ins = dve.tensor_copy(c32[:, :, t, :].rearrange("p b (j r) -> p b j r", r=2),
                                      ps[:, 0, 0:128].rearrange("p (b j t r) -> p b j t r", b=B, j=NJ, t=2)[:, :, :, t, :])
            link(ins)

            with dve.Fori(0, B) as b:
                n, off = number(b), before(b)
                base = off + 2 * b
                for half in range(2):
                    dve.wait_ge(s["q_scores"], 2 * base + half + 1)
                    dve.tensor_copy(mrun[:, half * GC:half * GC + GC],
                                    ps[:, 1 + 2 * half:3 + 2 * half, :].rearrange("p k n -> p (k n)")
                                    ).then_inc(s["q_max"], 1)
                with dve.Fori(0, n) as i:
                    u = base + i + 1
                    for half in range(2):
                        m = mrun[:, half * GC:half * GC + GC]
                        dve.wait_ge(s["q_scores"], 2 * u + half + 1)
                        dve.wait_ge(s["q_max"], 2 * u + half + 1)
                        dve.scalar_tensor_tensor(out=m, in0=ps[:, 1 + 2 * half:3 + 2 * half, :]
                                                 .rearrange("p k n -> p (k n)"),
                                                 scalar=mbias[:, bass.ds(NC * b + NC - 1 - i, 1)], in1=m,
                                                 op0=ALU.add, op1=ALU.max).then_inc(s["q_max"], 1)
                u = base + n + 1
                for half in range(2):
                    dve.wait_ge(s["q_scores"], 2 * u + half + 1)
                    dve.tensor_reduce(mall[:, half * HG:half * HG + HG],
                                      ps[:, 1 + 2 * half:3 + 2 * half, :].rearrange("p k (h n) -> p (k h) n", n=128),
                                      AX_X, ALU.max).then_inc(s["q_max"], 1)
                dve.wait_ge(s["q_max"], 2 * u + 4)
                dve.tensor_tensor(r32[:], c32[:, bass.ds(b, 1), :, :].rearrange("p o t h -> p (o t) h"),
                                  mall[:, None, :].broadcast_to([128, 2, H]), ALU.subtract).then_inc(s["r_seq"], 1)
                dve.wait_ge(s["r_seq"], 2 * b + 1)
                dve.wait_ge(s["rT_done"], b + 1)
                dve.tensor_scalar(rhl[:, 0, :, :], r32[:], SHIFT / XSCALE, None, ALU.add).then_inc(s["r_seq"], 1)
                dve.wait_ge(s["r_seq"], 2 * b + 2)
                dve.scalar_tensor_tensor(out=rhl[:, 1, :, :], in0=r32[:], scalar=SHIFT / XSCALE, in1=rhl[:, 0, :, :],
                                         op0=ALU.add, op1=ALU.subtract).then_inc(s["r_ready"], 1)

            def normalise(b, g):
                q = 2 * b + g
                dve.wait_ge(s["u_done"], q + 2)
                uv = ps[:, 6:8, 0:4 * (DH + 1)].rearrange("p k (h d) -> p k h d", h=4)
                dve.reciprocal(rinv[:].rearrange("p (k h) -> p k h", k=2), uv[:, :, :, DH]).then_inc(s["u_inv"], 1)
                dve.wait_ge(s["u_inv"], q + 1)
                dve.wait_ge(s["oT_fill"], q + 1)
                for k in range(2):
                    ins = dve.tensor_tensor(on[:, 4 * k:4 * k + 4, :], uv[:, k, :, 0:DH],
                                            rinv[:, 4 * k:4 * k + 4, None].broadcast_to([128, 4, DH]), ALU.mult)
                ins.then_inc(s["on_ready"], 1)

            def residual(b):
                dve.wait_ge(s["xo_done"], b + 2)
                row = xs[:, bass.ds(b, 1), :].rearrange("p o d -> p (o d)")
                dve.tensor_tensor(row, ps[:, 7, 0:128], row, ALU.add).then_inc(s["x1_done"], 1)

            def batch(b, first):
                n, off = number(b), before(b)
                for g in range(2):
                    base = 2 * (off + b) + g * (n + 1)

                    def split(u):
                        for k in range(2):
                            dve.wait_ge(s["exp_done"], 2 * u + k + 3)
                            dve.wait_ge(s["pv_done"], 2 * u + k + 1)
                            dve.tensor_copy(ph[:, k, :], p32[:, k, :]).then_inc(s["p_hi"], 1)
                            dve.wait_ge(s["p_hi"], 2 * u + k + 1)
                            dve.tensor_tensor(pl[:, k, :], p32[:, k, :], ph[:, k, :], ALU.subtract
                                              ).then_inc(s["p_ready"], 1)

                    def sums(t, count):
                        dve.wait_ge(s["t_hi"], 2 * (2 * b + g) + count)
                        dve.scalar_tensor_tensor(out=tl[:, t, :],
                                                 in0=ps[:, 2 + 2 * t:4 + 2 * t, :].rearrange("p k n -> p (k n)"),
                                                 scalar=TSCALE, in1=th[:, t, :], op0=ALU.mult, op1=ALU.subtract
                                                 ).then_inc(s["t_lo"], 1)

                    split(base)
                    if g == 1 or not first:
                        normalise(*((b, 0) if g == 1 else (b - 1, 1)))
                    split(base + 1)
                    sums(1, 1)
                    with dve.Fori(1, n) as i:
                        split(base + i + 1)
                    if g == 0 and not first:
                        residual(b - 1)
                    sums(0, 2)

            batch(0, True)
            with dve.Fori(1, B) as b:
                batch(b, False)
            normalise(B - 1, 1)
            residual(B - 1)

            dve.wait_ge(s["x1_done"], B + 1)
            norm(xs, 2).then_inc(s["lat_ready"], 1)
            dve.wait_ge(s["lat_ready"], 2)
            dve.wait_ge(s["late_in"], LATE)
            dve.wait_ge(s["const_done"], N_CONST)
            link(dve.tensor_tensor(xs[:], xs[:], abr[:, 1:2, :].broadcast_to([128, B, D]), ALU.add))
            dve.wait_ge(s["a_fill"], 1)
            dve.tensor_scalar(qTa, ps[:, 1, :], ab[:, 0:1], None, ALU.add)
            dve.tensor_tensor(va[:, :, :, 0:DK], ps[:, 3, :].rearrange("p (b h d) -> p b h d", b=B, h=AH)
                              if False else ps[:, 3, :].rearrange("p (b h d) -> p b h d", b=B, h=AH),
                              abr[:, 0, :].rearrange("p (h d) -> p h d", h=AH)[:, None, :, :]
                              .broadcast_to([128, B, AH, DK]), ALU.add)
            dve.memset(va[:, :, :, DK:DK + 1], 1.0)
            link(dve.tensor_scalar(kTa, ps[:, 2, :], ab[:, 1:2], None, ALU.add))
            for b in range(B):
                dve.tensor_tensor(kblk[:, b, :, :],
                                        kTa[:, None, b * 128:b * 128 + 128].broadcast_to([128, 4, 128]),
                                        headmask[:, :, None].broadcast_to([128, 4, 128]), ALU.mult
                                        ).then_inc(s["a_done"], 1)
            for k in range(4 * B + 2):
                if k < 4 * B:
                    b, g = k // 4, k % 4
                    dve.wait_ge(s["a_s"], k + 1)
                    link(dve.tensor_reduce(amax[:, b, 4 * g:4 * g + 4],
                                           ps[:, k % 3, :].rearrange("p (h k) -> p h k", h=4), AX_X, ALU.max))
                    dve.tensor_scalar(nmax[:, b, 4 * g:4 * g + 4], amax[:, b, 4 * g:4 * g + 4], -ASCALE, None,
                                      ALU.mult).then_inc(s["a_max"], 1)
                if 1 <= k <= 4 * B:
                    dve.wait_ge(s["a_tr"], k)
                    if k >= 5:
                        dve.wait_ge(s["a_pv"], k - 4)
                    c = 4 * ((k - 1) % 4)
                    dve.tensor_copy(paT[:, c:c + 4, :].rearrange("p h k -> p (h k)"), ps[:, 4 + (k - 1) % 2, :]
                                    ).then_inc(s["a_trc"], 1)
                if k % 4 == 1 and k >= 5:
                    b = (k - 5) // 4
                    dve.wait_ge(s["a_pv"], 4 * b + 4)
                    o = ps[:, 3 + 3 * (b % 2), 0:9 * AH].rearrange("p (h d) -> p h d", h=AH)
                    link(dve.reciprocal(ra, o[:, :, DK]))
                    if b >= 1:
                        dve.wait_ge(s["a_oT"], b)
                    dve.tensor_tensor(oa.rearrange("p (h d) -> p h d", h=AH), o[:, :, 0:DK],
                                      ra[:, :, None].broadcast_to([128, AH, DK]), ALU.mult).then_inc(s["a_o"], 1)
                if k % 4 == 0 and k >= 8:
                    b = (k - 8) // 4
                    dve.wait_ge(s["a_y"], b + 1)
                    dve.tensor_tensor(xs[:, b, :], ps[:, 7, 0:128], xs[:, b, :], ALU.add).then_inc(s["a_x2"], 1)
            dve.wait_ge(s["a_y"], B)
            dve.tensor_tensor(xs[:, B - 1, :], ps[:, 7, 0:128], xs[:, B - 1, :], ALU.add).then_inc(s["a_x2"], 1)

            dve.wait_ge(s["a_x2"], B)
            norm(xs, 3).then_inc(s["lat_ready"], 1)
            dve.wait_ge(s["lat_ready"], 3)
            dve.wait_ge(s["xT_done"], 2)
            dve.tensor_tensor(xTp[1], ps[:, 0, :], xTp[0], ALU.subtract).then_inc(s["xT_done"], 1)
            dve.wait_ge(s["r_log"], 1)
            logits = ps[:, 1, 0:B * E].rearrange("p (b e) -> p b e", b=B)
            link(dve.tensor_reduce(lgm, logits, AX_X, ALU.max))
            dve.tensor_tensor(lg, logits, lgm[:, :, None].broadcast_to([128, B, E]), ALU.subtract
                              ).then_inc(s["r_log"], 1)
            dve.wait_ge(s["r_log"], 2)
            other = lg[:, :, None, :].broadcast_to([128, B, E, E])
            own = lg[:, :, :, None].broadcast_to([128, B, E, E])
            g4 = gtm.rearrange("p (b e) f -> p b e f", b=B)
            e4 = eqm.rearrange("p (b e) f -> p b e f", b=B)
            dve.tensor_tensor(g4, other, own, ALU.is_gt)
            link(dve.tensor_tensor(e4, other, own, ALU.is_equal))
            link(dve.tensor_tensor(e4, e4, tri[:, None, :, :].broadcast_to([128, B, E, E]), ALU.mult))
            link(dve.tensor_tensor(gtm, gtm, eqm, ALU.add))
            dve.tensor_reduce(rank, gtm, AX_X, ALU.add)
            dve.wait_ge(s["r_exp"], 1)
            link(dve.tensor_reduce(sm, ex, AX_X, ALU.add))
            dve.reciprocal(sm, sm)
            link(dve.scalar_tensor_tensor(out=pr[:].rearrange("p b e -> p (b e)"), in0=rank, scalar=1.5,
                                          in1=ex[:].rearrange("p b e -> p (b e)"), op0=ALU.is_lt, op1=ALU.mult))
            link(dve.scalar_tensor_tensor(out=pr, in0=pr, scalar=0.5, in1=sm[:, :, None].broadcast_to([128, B, E]),
                                          op0=ALU.mult, op1=ALU.mult))
            def combine(e):
                dve.wait_ge(s["f_o"], e + 1)
                if e >= 1:
                    dve.wait_ge(s["f_acc"], B * e)
                for b in range(B):
                    dve.scalar_tensor_tensor(out=xs[:, b, :], in0=ps[:, 6 + e % 2, b * 128:b * 128 + 128],
                                             scalar=pr[:, b, e:e + 1], in1=xs[:, b, :],
                                             op0=ALU.mult, op1=ALU.add).then_inc(s["f_acc"], 1)

            for e in range(E):
                for c in (2 * e, 2 * e + 1):
                    bank = 2 + 2 * (c % 2)
                    dve.wait_ge(s["f_t"], c + 1)
                    if c >= 2:
                        dve.wait_ge(s["f_g"], c - 1)
                    link(dve.scalar_tensor_tensor(out=gg[:, c % 2, :], in0=tt[:, c % 2, :], scalar=1.0,
                                                  in1=ps[0:FH, bank, :], op0=ALU.add, op1=ALU.mult))
                    dve.tensor_tensor(gT[0:FH, c, :], gg[:, c % 2, :], ps[0:FH, bank + 1, :], ALU.mult
                                      ).then_inc(s["f_g"], 1)
                if e >= 1:
                    combine(e - 1)
            combine(E - 1)
            dve.wait_ge(s["f_acc"], B * E)
            dve.sem_inc(s["ready_out"], 1)


_INS = ["x", "ctx_1024", "mask_BxS2_bk0", "L0_xattn_g1", "L0_xattn_b1", "L0_xattn_g2", "L0_xattn_b2",
        "L0_xattn_Wq", "L0_xattn_Wkv", "L0_xattn_Wout", "L0_attn_Wq", "L0_attn_bq", "L0_attn_Wk",
        "L0_attn_bk", "L0_attn_Wv", "L0_attn_bv", "L0_attn_Wo", "L0_attn_bo", "L0_ffn_router_weight",
        "L0_ffn_w1", "L0_ffn_w2"]


def kernel(**inputs):
    import numpy as _np
    import concourse.bacc as _bacc
    from concourse import mybir as _mybir
    from concourse.bass_utils import run_bass_kernel_spmd as _run

    nc = _bacc.Bacc("TRN2", target_bir_lowering=False, num_devices=1)
    arrays, args = {}, []
    for name in _INS:
        a = _np.ascontiguousarray(inputs[name])
        arrays[f"in_{name}"] = a
        args.append(nc.dram_tensor(f"in_{name}", a.shape, _mybir.dt.from_np(a.dtype), kind="ExternalInput").ap())
    args.append(nc.dram_tensor("out_x", (4, 128, 128), F32, kind="ExternalOutput").ap())
    perceiver_block(nc, *args)
    r = _run(nc, [arrays], core_ids=[0])
    return r.results[0]["out_x"]
```

```python
from contextlib import ExitStack

import concourse.bass as bass
from concourse import mybir

ALU = mybir.AluOpType
ACT = mybir.ActivationFunctionType
AX_X = mybir.AxisListType.X
F32 = mybir.dt.float32
F16 = mybir.dt.float16
BF16 = mybir.dt.bfloat16
I32 = mybir.dt.int32
U8 = mybir.dt.uint8

EPS = 1e-5
MASKED = -1e30
OUTSIDE = 3e9
WINDOW = 32


def perceiver_block(nc, x, ctxt, mask, g1, b1, g2, b2, Wq, Wkv, Wout,
                    aWq, abq, aWk, abk, aWv, abv, aWo, abo, rw, w1, w2, out):
    B, L, D = x.shape
    S = ctxt.shape[1]
    INNER = Wq.shape[1]
    DH = 64
    H = INNER // DH
    NC = S // 128
    NP = NC // 2
    NJ = INNER // 128
    HG = H // 2
    GC = HG * L
    QB = H * L
    E, _, F2 = w1.shape
    F = F2 // 2
    FH = F // 2
    AH = 16
    DK = D // AH
    ASCALE = DK ** -0.5
    XSCALE = 1.0 / 8.0
    SHIFT = 4.0
    TSCALE = 2.0 ** -5
    BL = B * L
    GROUPS = (range(B - 1), range(B - 1, B))

    with ExitStack() as ctx:
        def sb(name, shape, dt):
            return ctx.enter_context(nc.sbuf_tensor(name, shape, dt))

        def sem(name):
            return ctx.enter_context(nc.semaphore(name))

        ps = ctx.enter_context(nc.psum_tensor("ps", [128, 8, 512], F32))

        ident = sb("ident", [128, 128], F32)
        identh = sb("identh", [128, 128], F16)
        identb = sb("identb", [128, 128], BF16)
        fold = sb("fold", [128, 128], F32)
        gt = sb("gt", [128, 2, 128], F32)
        gb = sb("gb", [128, 4], F32)
        zero2 = sb("zero2", [128, 130], F16)
        neghalf = sb("neghalf", [128, NC], F32)
        weight = sb("weight", [1, B * NP], F32)
        band = sb("band", [128, 128], BF16)
        tri = sb("tri", [128, 8, 8], F32)
        mk = sb("mk", [B * NP, 256], U8)
        mkf = sb("mkf", [B * NP, 256], F32)
        mkb = sb("mkb", [128, 256], BF16)
        flag = sb("flag", [B * NP, 1], F32)
        lastc = sb("lastc", [1, B * NP], F32)
        metaf = sb("metaf", [1, 12], F32)
        place = sb("place", [1, 3, B], F32)
        packf = sb("packf", [1, 3], F32)
        pack = sb("pack", [1, 3], I32)
        mbc = sb("mbc", [128, B, NP, 2], F32)
        xs = sb("xs", [128, B, D], F32)
        xn = sb("xn", [128, B, D], F32)
        st = sb("st", [128, 2, NC, 6], F32)
        mv = sb("mv", [128, 2, NC, 2], F32)
        rs = sb("rs", [128, 2, NC], F32)
        stl = sb("stl", [128, B, 6], F32)
        mvl = sb("mvl", [128, B, 2], F32)
        rsl = sb("rsl", [128, B], F32)
        zl = sb("zl", [128, B, 2, 128], F16)
        zlT = sb("zlT", [128, 2, B, 128], F16)
        zc = sb("zc", [128, B * NC, 2, 128], F16)
        zcT = sb("zcT", [128, B * NC, 2, 128], F16)
        raw = sb("raw", [128, 2, NC, 128], F32)
        raw_pairs = raw[:].rearrange("p s (i c) k -> p s i c k", c=2)
        zc_pairs = zc[:].rearrange("p (i c) a k -> p i c a k", c=2)
        zcT_pairs = zcT[:].rearrange("p (i c) a k -> p i c a k", c=2)
        qq = sb("qq", [128, 2, 2, B, QB], F16)
        reg = sb("reg", [128, 9216], F32)
        wq_s = reg[:, 0:1024]
        wkv_s = reg[:, 1024:3072]
        wk2 = [w.rearrange("p (h t a) -> p h t a", h=H, t=2)
               for w in (reg[:, 3072:5120].bitcast(F16),
                         zcT[:].rearrange("p u a k -> p (u a k)")[:, 2 * INNER:6 * INNER])]
        q2 = reg[:, 5120:9216].bitcast(F16).rearrange("p (h n) -> p h n", h=H)
        wqt = zcT[:].rearrange("p u a k -> p (u a k)")[:, 0:2 * INNER].rearrange("p (a n) -> p a n", a=2)
        p32 = reg[:, 0:1024].rearrange("p (j n) -> p j n", j=2)
        ph = reg[:, 1024:1536].bitcast(F16).rearrange("p (j n) -> p j n", j=2)
        pl = reg[:, 1536:2048].bitcast(F16).rearrange("p (j n) -> p j n", j=2)
        th = reg[:, 2048:3072].bitcast(F16).rearrange("p (t n) -> p t n", t=2)
        tl = reg[:, 3072:4096].bitcast(F16).rearrange("p (t n) -> p t n", t=2)
        on = reg[:, 4096:4608].rearrange("p (h d) -> p h d", h=HG)
        oT = reg[:, 4608:5632].rearrange("p (j n) -> p j n", j=NJ)
        rT = reg[0:64, 5632:5696].bitcast(F16)
        pick = reg[:, 6100:7124].bitcast(F16).rearrange("p (t k g m r d) -> p t k g m r d", t=2, k=2, g=4, m=4, r=4)
        mbias = reg[:, 6000:6000 + B * NC]
        mt = [reg[:, c:c + (NP + 1) * H].rearrange("p (u h) -> p u h", h=H) for c in (5696, 6400)]
        rinv = sb("rinv", [128, HG], F32)
        wv = sb("wv", [128, 2, 2, H, DH + 1], F16)
        cw = sb("cw", [128, H, 2, 2], F16)
        wo_s = sb("wo_s", [128, NJ, D], F32)
        c32 = reg[:, 6100:6100 + B * 2 * H].rearrange("p (b t h) -> p b t h", b=B, t=2)
        mall = sb("mall", [128, H], F32)
        r32 = sb("r32", [128, 2, H], F32)
        rhl = sb("rhl", [128, 2, 2, H], F16)
        rawflat = raw[:].rearrange("p s c k -> p (s c k)")
        w1_s = rawflat[:, 0:E * F2].rearrange("p (e f) -> p e f", e=E)
        aw = rawflat[:, 2816:3328].rearrange("p (k n) -> p k n", k=4)
        abr = rawflat[:, 3328:3584].rearrange("p (k n) -> p k n", k=2)
        rw_s = rawflat[:, 3584:3592]
        ab = rawflat[:, 3592:3595]
        late = qq[:].rearrange("p a t b n -> p (a t b n)").bitcast(F32)
        xT = late[:, 0:512]
        qk32 = late[:, 512:1536].rearrange("p (t n) -> p t n", t=2)
        qks = late[:, 1536:3584].bitcast(F16).rearrange("p (t g n) -> p t g n", t=2, g=4)
        qkh, qkl = [late[:, c:c + 512].bitcast(F16).rearrange("p (t n) -> p t n", t=2) for c in (9304, 9816)]
        kblk = late[:, 12288:16384].bitcast(F16).rearrange("p (g b m n) -> p g b m n", g=4, b=B, m=4)
        va = late[:, 3584:4160].rearrange("p (b h d) -> p b h d", b=B, h=AH)
        vap = [late[:, c:c + 288].bitcast(F16).rearrange("p (b h d) -> p b h d", b=B, h=AH) for c in (10328, 10616)]
        amin = late[:, 4160:4224].rearrange("p (b h) -> p b h", b=B)
        pa = late[:, 4288:6336].rearrange("p (h k) -> p h k", h=AH)
        paT = [late[:, c:c + 1024].bitcast(F16).rearrange("p (h k) -> p h k", h=AH) for c in (6336, 7360)]
        ra = late[:, 8384:8400]
        oa = late[:, 8400:8528]
        oaT = late[:, 8528:8656]
        lg = late[:, 8656:8688].rearrange("p (b e) -> p b e", b=B)
        lgm = late[:, 8688:8692]
        ex = late[:, 8692:8724].rearrange("p (b e) -> p b e", b=B)
        sm = late[:, 8724:8728]
        gtm = late[:, 8728:8984].rearrange("p (b f) -> p b f", f=E)
        eqm = late[:, 8984:9240].rearrange("p (b f) -> p b f", f=E)
        rank = late[:, 9240:9272]
        pr = late[:, 9272:9304].rearrange("p (b e) -> p b e", b=B)
        tt = late[0:FH, 9304:10328].rearrange("p (k n) -> p k n", k=2)
        gg = late[0:FH, 10328:11352].rearrange("p (k n) -> p k n", k=2)
        w2_s = reg[0:FH, 7168:9216].rearrange("p (c d) -> p c d", c=2 * E)
        w1p = [zcT[:].rearrange("p u a k -> p (u a k)")[:, k * E * F2:(k + 1) * E * F2]
               .rearrange("p (e f) -> p e f", e=E) for k in range(2)]
        xTp = [late[:, 11352 + 256 * k:11608 + 256 * k].bitcast(F16) for k in range(2)]
        gT = zc[:].rearrange("p u a k -> p (u a k)").bitcast(F32)[:, 0:8192].rearrange(
            "p (c n) -> p c n", c=2 * E)

        names = """mb_turned a_trh xp_done k_clear k_block qk_split q_stacked k_stacked qk_fill va_done nb_done
            qk_32 gb2_in mask_in x_in gb_in wk_in wv_in wq_in w_split wo_in late_in ctx_in0 ctx_in1
            const_done pool_fold fl_done cnt_done meta_done mb_done seq gt_done stat_ready rs_ready
            lat_ready fill hi lo c_done c_used ctx_rs z_ready zT_fill zT_copied slab_free q_scores q_max
            r_ready rT_done rT_copied row_set sc_ready exp_done p_ready pv_done t_hi t_lo u_done on_ready
            oT_fill oT_copied xo_done x1_done xT_fill xT_done ctx_bn z_full z_hi r_seq p_hi u_inv passed_dve
            passed_pool passed_sp passed_pe passed_act a_fill a_s a_max a_exp a_tr a_trc a_pv a_o a_oT a_oTc
            a_y a_x2 r_log r_exp f_y f_t f_g f_o f_acc out_sent ready_out""".split()
        s = {n: sem(n) for n in names}

        mask_rows = mask.rearrange("b (c k) -> (b c) k", c=NP)
        x_rows = x.rearrange("b l d -> l b d")
        out_rows = out.rearrange("b l d -> l b d")
        ctx_rows = ctxt.rearrange("b (p c k) d -> b p k c d", p=NP, c=2)

        T_WK, T_WQ, T_LT, T_WV, T_QT, T_QQ = 0, 4, 5, 6, 8, 16
        N_FILL = T_QQ + H
        TURNED = [[(bank, slice(g[0] * 128, g[-1] * 128 + 128)) for bank, g in zip(banks, GROUPS)]
                  for banks in ((0, 3), (1, 0))]
        block = ctx.enter_context(nc.Block())

        def counts(eng):
            n = eng.value_load(pack[0:1, 0:1], min_val=0, max_val=2 ** 24)
            off = eng.value_load(pack[0:1, 1:2], min_val=0, max_val=2 ** 24)
            return (lambda b: nc.s_assert_within(eng.snap((n >> (b * 6)) & 63), 2, NC, skip_runtime_bounds_check_because="clamped when packed"),
                    lambda b: nc.s_assert_within(eng.snap((off >> (b * 6)) & 63), 0, 3 * NC, skip_runtime_bounds_check_because="clamped when packed"),
                    lambda b: nc.s_assert_within(eng.snap((n >> (b * 6 + 1)) & 31), 1, NP, skip_runtime_bounds_check_because="clamped when packed"),
                    lambda b: nc.s_assert_within(eng.snap((off >> (b * 6 + 1)) & 31), 0, 3 * NP, skip_runtime_bounds_check_because="clamped when packed"))

        def prepared(e, part):
            src = ps[:, 2 * (e % 4):2 * (e % 4) + 2, :]
            flat = src.rearrange("p k n -> p (k n)")
            if e < T_WQ:
                return wk2[part][:, 4 * e:4 * e + 4, :, :].rearrange("p h t a -> p (h t a)"), flat
            if e == T_WQ:
                return wqt[:, part, :], flat
            if T_WV <= e < T_QT:
                return wv[:, part, e - T_WV, :, 0:DH], src.rearrange("p k (h d) -> p (k h) d", h=8)
            if e == T_LT:
                return zlT[:].rearrange("p a b l -> p (a b l)"), src[:, 0, :].bitcast(F16)
            if e < T_QQ:
                k = 2 * (e - T_QT)
                rows = slice(64 * part, 128)
                return q2[rows, k:k + 2, :].rearrange("p h n -> p (h n)"), flat[rows]
            h = e - T_QQ
            return (qq[:, part, :, :, h * 128:h * 128 + 128],
                    src.rearrange("p t (b l) -> p t b l", b=B))

        @block.sync
        def _(sp):
            sp.sem_inc(s["row_set"], 64)
            sp.dma_start(mk[:], mask_rows).then_inc(s["mask_in"], 16)
            sp.dma_start(wkv_s[:, 0:INNER], Wkv[:, 0:INNER]).then_inc(s["wk_in"], 16)
            sp.dma_start(xs[:], x_rows).then_inc(s["x_in"], 16)
            sp.dma_start(wq_s, Wq).then_inc(s["wq_in"], 16)
            sp.dma_start(wkv_s[:, INNER:], Wkv[:, INNER:]).then_inc(s["wv_in"], 16)
            sp.dma_start(wo_s[:], Wout.rearrange("(j p) d -> p j d", p=128)).then_inc(s["wo_in"], 16)
            sp.wait_ge(s["meta_done"], 1)
            _, _, pairs, _ = counts(sp)
            with sp.Fori(0, B // 2) as pair:
                for par in range(2):
                    b = 2 * pair + par
                    n = pairs(b)
                    sp.wait_ge(s["slab_free"], b + 1)
                    sp.sem_inc(s["passed_sp"], 1)
                    with sp.Fori(0, n) as i:
                        sp.dma_start(raw_pairs[:, par, bass.ds(i, 1), :, :].rearrange("p o c d -> p (o c) d"),
                                     ctx_rows[bass.ds(b, 1), bass.ds(NP - 1 - i, 1), :, :, :]
                                     .rearrange("a o k c d -> (a o k) c d")).then_inc(s[f"ctx_in{par}"], 16)
            sp.wait_ge(s["slab_free"], B + 2)
            sp.dma_start(w1_s, w1.rearrange("e h f -> h e f")).then_inc(s["late_in"], 16)
            for b in range(B):
                sp.wait_ge(s["rT_copied"], b + 2)
                for k in range(4):
                    sp.dma_start(qq[127:128, k // 2, k % 2, b, :].rearrange("p (h l) -> p h l", h=H),
                                 rT[H * k:H * k + H, :]).then_inc(s["row_set"], 16)
            sp.wait_ge(s["c_done"], 1)
            sp.dma_start(w2_s, w2.rearrange("e (c f) d -> f (e c) d", c=2)).then_inc(s["late_in"], 16)
            sp.dma_start(rw_s, rw).then_inc(s["late_in"], 16)
            for k, w in enumerate((aWq, aWk, aWv, aWo)):
                sp.dma_start(aw[:, k, :], w).then_inc(s["late_in"], 16)
            for k, v in enumerate((abq, abk)):
                sp.dma_start(ab[:, k:k + 1], v.rearrange("(p o) -> p o", o=1)).then_inc(s["late_in"], 16)
            for k, v in enumerate((abv, abo)):
                sp.dma_start(abr[:, k, :], v.rearrange("(o d) -> o d", o=1).broadcast_to([128, 128])
                             ).then_inc(s["late_in"], 16)
            sp.wait_ge(s["ready_out"], 1)
            sp.dma_start(out_rows, xs[:]).then_inc(s["out_sent"], 16)
            sp.wait_ge(s["out_sent"], 16)
        LATE = 16 * 11

        @block.gpsimd
        def _(pool):
            order = [0]

            def link(ins):
                order[0] += 1
                ins.then_inc(s["const_done"], 1)
                pool.wait_ge(s["const_done"], order[0])

            pool.dma_start(gb[:, 3:4], b2.rearrange("(p o) -> p o", o=1)).then_inc(s["gb2_in"], 16)
            link(pool.memset(ident[:], 0.0))
            link(pool.affine_select(out=ident[:], in_=ident[:], compare_op=ALU.not_equal, fill=1.0,
                                    base=0, pattern=[[-1, 128]], channel_multiplier=1))
            link(pool.iota(weight[:].rearrange("p (b c) -> p b c", b=B), [[0, B], [-2, NP]], base=NC,
                           channel_multiplier=0, allow_small_or_imprecise_dtypes=True))
            link(pool.affine_select(out=fold[:], in_=ident[:], compare_op=ALU.not_equal, fill=-1.0,
                                    base=-127, pattern=[[0, 128]], channel_multiplier=1))
            link(pool.tensor_copy(identh[:], ident[:]))
            link(pool.memset(neghalf[:], -0.5))
            pool.memset(zero2[:], 0.0).then_inc(s["pool_fold"], 1)
            pool.memset(wv[:], 0.0).then_inc(s["pool_fold"], 1)
            pool.wait_ge(s["pool_fold"], 2)
            for t in range(2):
                pool.affine_select(out=wv[:, 0, t, :, DH], in_=wv[:, 0, t, :, DH],
                                   compare_op=ALU.not_equal, fill=1.0, base=-127, pattern=[[0, H]],
                                   channel_multiplier=1).then_inc(s["pool_fold"], 1)
            for k in range(2):
                pool.wait_ge(s["stat_ready"], k + 1)
                pool.tensor_tensor(rsl[:], rsl[:], neghalf[:, 0:B], ALU.pow).then_inc(s["rs_ready"], 1)
            link(pool.memset(band[:], 0.0))
            link(pool.affine_select(out=band[:], in_=band[:], compare_op=ALU.is_ge, fill=OUTSIDE,
                                    base=WINDOW // 2, pattern=[[-1, 128]], channel_multiplier=1))
            link(pool.affine_select(out=band[:], in_=band[:], compare_op=ALU.is_ge, fill=OUTSIDE,
                                    base=WINDOW // 2, pattern=[[1, 128]], channel_multiplier=-1))
            link(pool.tensor_copy(identb[:], ident[:]))
            link(pool.memset(tri[:], 1.0))
            link(pool.affine_select(out=tri[:], in_=tri[:], compare_op=ALU.is_gt, fill=0.0, base=0,
                                    pattern=[[1, E], [-1, E]], channel_multiplier=0))
            _, _, pairs, pairs_before = counts(pool)
            with pool.Fori(0, B // 2) as half:
                for par in range(2):
                    b = 2 * half + par
                    n, off = pairs(b), pairs_before(b)
                    even, odd = [[st[:, par, :, 3 * k + f] for f in range(3)] for k in range(2)]
                    mean, diff, var = mv[:, par, :, 0], mv[:, par, :, 1], rs[:, par, :]
                    pool.wait_ge(s["ctx_bn"], off + n)
                    pool.sem_inc(s["passed_pool"], 1)
                    pool.tensor_tensor(diff, even[1], odd[1], ALU.subtract).then_inc(s["ctx_rs"], 1)
                    pool.tensor_tensor(mean, even[1], odd[1], ALU.add).then_inc(s["ctx_rs"], 1)
                    pool.tensor_tensor(var, even[2], odd[2], ALU.add).then_inc(s["ctx_rs"], 1)
                    pool.wait_ge(s["ctx_rs"], 8 * b + 3)
                    pool.tensor_tensor(diff, diff, diff, ALU.mult).then_inc(s["ctx_rs"], 1)
                    pool.tensor_scalar(var, var, 1.0 / D, EPS, ALU.mult, ALU.add)
                    pool.wait_ge(s["ctx_rs"], 8 * b + 4)
                    pool.sem_inc(s["passed_pool"], 1)
                    pool.tensor_scalar(diff, diff, 0.25, None, ALU.mult).then_inc(s["ctx_rs"], 1)
                    pool.tensor_scalar(mean, mean, 0.5, None, ALU.mult)
                    pool.wait_ge(s["ctx_rs"], 8 * b + 5)
                    pool.tensor_tensor(var, var, diff, ALU.add).then_inc(s["ctx_rs"], 1)
                    pool.memset(raw[:, par, :, 127:128], 1.0).then_inc(s["ctx_rs"], 1)
                    pool.wait_ge(s["ctx_rs"], 8 * b + 7)
                    pool.sem_inc(s["passed_pool"], 1)
                    pool.tensor_tensor(var, var, neghalf[:, 0:NC], ALU.pow).then_inc(s["ctx_rs"], 1)
                    pool.wait_ge(s["ctx_rs"], 8 * b + 8)
                    pool.sem_inc(s["passed_pool"], 1)
                    with pool.Fori(0, n) as i:
                        rows = raw_pairs[:, par, bass.ds(i, 1), :, :].rearrange("p o c k -> p (o c) k")
                        u = off + i
                        hi, lo = [zc_pairs[:, bass.ds(u, 1), :, k, :].rearrange("p o c k -> p (o c) k") for k in range(2)]
                        mean, scale = [v.rearrange("p s (i c) -> p s i c", c=2)[:, par, bass.ds(i, 1), :]
                                       .rearrange("p o c -> p (o c)")[:, :, None].broadcast_to([128, 2, 127])
                                       for v in (mv[:, :, :, 0], rs[:])]
                        pool.tensor_tensor(rows[:, :, 0:127], rows[:, :, 0:127], mean, ALU.subtract
                                           ).then_inc(s["z_full"], 1)
                        pool.wait_ge(s["z_full"], 2 * u + 1)
                        pool.tensor_tensor(rows[:, :, 0:127], rows[:, :, 0:127], scale, ALU.mult
                                           ).then_inc(s["z_full"], 1)
                        pool.wait_ge(s["z_full"], 2 * u + 2)
                        pool.tensor_copy(hi, rows).then_inc(s["z_hi"], 1)
                        pool.wait_ge(s["z_hi"], u + 1)
                        pool.tensor_tensor(lo, rows, hi, ALU.subtract).then_inc(s["z_ready"], 1)
                    pool.wait_ge(s["z_ready"], off + n)
                    pool.sem_inc(s["slab_free"], 1)
            pool.wait_ge(s["r_ready"], B)
            link(pool.memset(pick, 0.0))
            for t in range(2):
                for k in range(2):
                    first, stride = ((2 * k, 1), (k, 2))[t]
                    link(pool.tensor_copy(pick[:, t, k, :, :, first:first + stride + 1:stride, :]
                                          .rearrange("p g m r d -> p (g m) r d"),
                                          identh[:].rearrange("p (h r d) -> p h r d", r=1, d=DK)
                                          .broadcast_to([128, AH, 2, DK])))
            for k in range(2):
                for batches in GROUPS:
                    pool.wait_ge(s["stat_ready"], 3 + 2 * k + (batches[0] > 0))
                    group = slice(batches[0], batches[-1] + 1)
                    pool.tensor_tensor(rsl[:, group], rsl[:, group], neghalf[:, group], ALU.pow
                                       ).then_inc(s["rs_ready"], 1)
                if k == 0:
                    pool.wait_ge(s["late_in"], LATE)
                    for e in range(E):
                        pool.tensor_copy(w1p[0][:, e, :], w1_s[:, e, :]).then_inc(s["w_split"], 1)
                        pool.wait_ge(s["w_split"], 2 * e + 1)
                        pool.tensor_tensor(w1p[1][:, e, :], w1_s[:, e, :], w1p[0][:, e, :], ALU.subtract
                                           ).then_inc(s["w_split"], 1)
        N_CONST = 6 + 5 - 1 + 2 + 5

        @block.tensor
        def _(pe):
            def half(e, k):
                return ps[:, 2 * (e % 4) + k, :]

            pe.wait_ge(s["const_done"], 5)
            pe.wait_ge(s["fl_done"], 3)
            pe.matmul(ps[0:1, 6, 0:B * NP], flag[:], ident[0:B * NP, 0:B * NP], start=True, stop=True)
            for c in range(2):
                mm = pe.transpose(ps[:, 7, c * B * NP:(c + 1) * B * NP], mkf[:, c * 128:c * 128 + 128],
                                  ident[0:B * NP, 0:B * NP])
            mm.then_inc(s["cnt_done"], 1)
            pe.wait_ge(s["gt_done"], 1)
            pe.wait_ge(s["wk_in"], 16)
            for h in range(H):
                e = T_WK + h // 4
                if h == 12:
                    pe.wait_ge(s["meta_done"], 1)
                    pe.wait_ge(s["mb_done"], 2)
                for r in range(0, 128, DH):
                    mm = pe.matmul(half(e, h // 2 % 2)[r:r + DH, h % 2 * 256:h % 2 * 256 + 256],
                                   wkv_s[:, h * DH:h * DH + DH],
                                   gt[:].rearrange("p t a -> p (t a)"), start=True, stop=True)
                if h % 4 == 3:
                    mm.then_inc(s["fill"], 1)
            pe.wait_ge(s["wq_in"], 16)
            pe.wait_ge(s["lo"], T_WQ - 3)
            for k in range(2):
                mm = pe.matmul(half(T_WQ, k), gt[:, 1, :], wq_s[:, k * 512:k * 512 + 512], start=True, stop=True)
            mm.then_inc(s["fill"], 1)
            number, before, pairs, pairs_before = counts(pe)
            pe.wait_ge(s["lat_ready"], 1)
            pe.wait_ge(s["lo"], T_LT - 3)
            for hl in range(2):
                for b in range(B):
                    c = (hl * B + b) * 128
                    mm = pe.transpose(half(T_LT, 0).bitcast(F16)[:, c:c + 128], zl[:, b, hl, :], identh[:])
            mm.then_inc(s["fill"], 1)
            pe.wait_ge(s["wv_in"], 16)
            for t in range(2):
                e = T_WV + t
                pe.wait_ge(s["lo"], e - 3)
                for k in range(2):
                    mm = pe.matmul(half(e, k), gt[:, t, :], wkv_s[:, INNER + k * 512:INNER + k * 512 + 512],
                                   start=True, stop=True)
                mm.then_inc(s["fill"], 1)

            def three(dst, ah, al, bh, bl):
                pe.matmul(dst, ah, bh, start=True, stop=False)
                pe.matmul(dst, ah, bl, start=False, stop=False)
                return pe.matmul(dst, al, bh, start=False, stop=True)

            latT = [zlT[:, k, :, :].rearrange("p b l -> p (b l)") for k in range(2)]
            pe.wait_ge(s["lo"], T_LT + 1)
            for h in range(H):
                e = T_QT + h // 2
                if h % 2 == 0 and e - 3 > T_LT + 1:
                    pe.wait_ge(s["lo"], e - 3)
                w = [wqt[:, k, h * DH:h * DH + DH] for k in range(2)]
                for k, m in ((0, 0), (0, 1), (1, 0)):
                    for r in range(0, 128, DH):
                        mm = pe.matmul(half(e, h % 2)[r:r + DH, :], w[k], latT[m], start=k + m == 0, stop=k == 1,
                                       skip_group_check=True)
                if h % 2 == 1:
                    mm.then_inc(s["fill"], 1)
            for h in range(H):
                e = T_QQ + h
                pe.wait_ge(s["lo"], e - 3)
                for t in range(2):
                    for k in range(2):
                        mm = pe.matmul(half(e, t), wk2[k][:, h, t, :], q2[:, h, :], start=(k == 0), stop=(k == 1))
                mm.then_inc(s["fill"], 1)

            def turn_pair(u):
                pe.wait_ge(s["z_ready"], u + 1)
                for c in range(2):
                    pe.wait_ge(s["zT_copied"], 2 * u + c + 1)
                    for hl in range(2):
                        mm = pe.transpose(ps[:, c, :].bitcast(F16)[:, hl * 128:hl * 128 + 128],
                                          zc_pairs[:, bass.ds(u, 1), c, hl, :].rearrange("p o d -> p (o d)"), identh[:])
                    mm.then_inc(s["zT_fill"], 1)

            def turn_pairs(b):
                n, off = pairs(b), pairs_before(b)
                with pe.Fori(0, n) as i:
                    turn_pair(off + i)

            def turn_shifts(b):
                pe.wait_ge(s["r_ready"], b + 1)
                pe.wait_ge(s["rT_copied"], b + 1)
                pe.sem_inc(s["passed_pe"], 1)
                pe.transpose(ps[0:64, 3, :].bitcast(F16)[:, 0:128],
                             rhl[:].rearrange("p a t h -> p (a t h)"), identh[:]).then_inc(s["rT_done"], 1)

            def maxima(b, first, last):
                n, off = pairs(b), pairs_before(b)
                base = 4 * off + 2 * b

                def query(h, t):
                    c = h * 128
                    return qq[:, 0, t, bass.ds(b, 1), c:c + 128].rearrange("p o n -> p (o n)")

                def latent_step(k):
                    pe.wait_ge(s["q_max"], base + k + 1)
                    keys = zlT[:, 0, bass.ds(b, 1), :].rearrange("p o d -> p (o d)")
                    for m in range(8):
                        mm = pe.matmul(ps[:, 4 + 2 * k + m // 4, m % 4 * 128:m % 4 * 128 + 128], query(8 * k + m, 1), keys,
                                       start=m % 4 == 0, stop=m % 4 == 3, skip_group_check=True)
                    mm.then_inc(s["q_scores"], 1)

                def pair(i):
                    pe.wait_ge(s["zT_copied"], 2 * (off + i) + 4)
                    pe.sem_inc(s["passed_pe"], 1)
                    keys = zcT_pairs[:, bass.ds(off + i, 1), :, 0, :].rearrange("p o c d -> p (o c) d")
                    for k in range(4):
                        pe.wait_ge(s["q_max"], base + 4 * i + k + 3)
                        for j in range(2):
                            bank = ps[:, 4 + 2 * (k % 2) + j, :]
                            for m in range(2):
                                pe.matmul(bank[:, m * 256:m * 256 + 256], query(4 * k + 2 * j + m, 0), keys,
                                          start=m == 0, stop=False, skip_group_check=True)
                            mm = pe.matmul(bank, identb[:, bass.ds(NP * b + NP - 1 - i, 1)].broadcast_to([128, 128]),
                                           mkb[:, None, :].broadcast_to([128, 2, 256]), start=False, stop=True,
                                           skip_group_check=True)
                        mm.then_inc(s["q_scores"], 1)

                latent_step(0)
                latent_step(1)
                with pe.Fori(0, n) as i:
                    pair(i)
                if not first:
                    turn_shifts(b - 1)
                if not last:
                    turn_pairs(b + 1)

            pe.wait_ge(s["lo"], N_FILL - 2)
            turn_pairs(0)
            pe.wait_ge(s["c_used"], 2)
            for b in range(B):
                for h in range(H):
                    c = (b * H + h) * 4
                    mm = pe.matmul(ps[:, 2, c:c + 4], q2[:, h, b * 128:b * 128 + 128],
                                   cw[:, h, :, :].rearrange("p k t -> p (k t)"), start=True, stop=True)
            mm.then_inc(s["c_done"], 1)
            pe.wait_ge(s["lo"], N_FILL)
            for b in range(B):
                maxima(b, b == 0, b == B - 1)

            SC, T1, T2, UB = 0, 2, 4, 6

            def at(tile, hl, idx):
                if tile is zlT:
                    return tile[:, hl, bass.ds(idx, 1), :].rearrange("p o d -> p (o d)")
                return tile[:, bass.ds(idx, 1), hl, :].rearrange("p o d -> p (o d)")

            def head_values(b, g):
                q = 2 * b + g
                pe.wait_ge(s["t_lo"], 2 * q + 4)
                pe.wait_ge(s["oT_copied"], q + 1)
                pe.wait_ge(s["x1_done"], b + 1)
                for h in range(HG):
                    o = ps[:, UB + h // 4, (h % 4) * (DH + 1):(h % 4 + 1) * (DH + 1)]
                    c = h * 128
                    step = 0
                    for t in range(2):
                        for a, w in ((th, 0), (th, 1), (tl, 0)):
                            mm = pe.matmul(o, a[:, t, c:c + 128], wv[:, w, t, g * HG + h, :],
                                           start=(step == 0), stop=(step == 5))
                            step += 1
                mm.then_inc(s["u_done"], 1)

            def turn_heads(b, g):
                pe.wait_ge(s["on_ready"], 2 * b + g + 1)
                for k in range(4):
                    mm = pe.transpose(ps[:, UB, k * 128:k * 128 + 128],
                                      on[:, 2 * k:2 * k + 2, :].rearrange("p h d -> p (h d)"), ident[:])
                mm.then_inc(s["oT_fill"], 1)

            def project(b):
                pe.wait_ge(s["oT_copied"], 2 * b + 3)
                for j in range(NJ):
                    mm = pe.matmul(ps[:, UB + 1, 0:128], oT[:, j, :], wo_s[:, j, :],
                                   start=(j == 0), stop=(j == NJ - 1))
                mm.then_inc(s["xo_done"], 1)

            def scores(b, g, zT, t, u):
                for k in range(2):
                    pe.wait_ge(s["exp_done"], 2 * u + k + 1)
                    c = g * GC + k * 512
                    rhs = [qq[:, a, t, bass.ds(b, 1), c:c + 512].rearrange("p o n -> p (o n)")
                           for a in range(2)]
                    three(ps[:, SC + k, :], zT[0], zT[1], rhs[0], rhs[1]).then_inc(s["sc_ready"], 1)

            def latent_scores(b, g, u):
                if g == 0:
                    pe.wait_ge(s["row_set"], 64 * b + 128)
                    pe.sem_inc(s["passed_pe"], 1)
                scores(b, g, [at(zlT, 0, b), at(zlT, 1, b)], 1, u)

            def values(z, dst, u, alone):
                for k in range(2):
                    pe.wait_ge(s["p_ready"], 2 * u + k + 3)
                    d = ps[:, dst + k, :]
                    pe.matmul(d, z[0], ph[:, k, :], start=alone, stop=False, skip_group_check=True)
                    pe.matmul(d, z[0], pl[:, k, :], start=False, stop=False, skip_group_check=True)
                    mm = pe.matmul(d, z[1], ph[:, k, :], start=False, stop=alone, skip_group_check=True)
                    mm.then_inc(s["pv_done"], 1)

            def batch(b, first, last):
                n, off = number(b), before(b)
                for g in range(2):
                    base = 2 * (off + b) + g * (n + 1)
                    group_before = (b, 0) if g == 1 else (b - 1, 1)
                    scores(b, g, [at(zcT, 0, off), at(zcT, 1, off)], 0, base + 1)
                    if first and g == 0:
                        turn_shifts(B - 1)
                    pe.wait_ge(s["t_lo"], 2 * (2 * b + g) + 1)
                    values([at(zl, 0, b), at(zl, 1, b)], T2, base, True)
                    if g == 1 or not first:
                        head_values(*group_before)
                    if first and g == 0:
                        pe.wait_ge(s["rT_copied"], B + 1)
                    for k in range(2):
                        pe.matmul(ps[:, T1 + k, 0:2], zero2[:, 0:128], zero2[:, 128:130],
                                  start=True, stop=False, skip_group_check=True)
                    with pe.Fori(1, n) as i:
                        scores(b, g, [at(zcT, 0, off + i), at(zcT, 1, off + i)], 0, base + i + 1)
                        values([at(zc, 0, off + i - 1), at(zc, 1, off + i - 1)], T1, base + i, False)
                    if g == 0:
                        latent_scores(b, 1, base + n + 1)
                    elif not last:
                        latent_scores(b + 1, 0, base + n + 1)
                    if g == 1 or not first:
                        turn_heads(*group_before)
                    values([at(zc, 0, off + n - 1), at(zc, 1, off + n - 1)], T1, base + n, False)
                    if g == 0 and not first:
                        project(b - 1)

            pe.wait_ge(s["wo_in"], 16)
            latent_scores(0, 0, 0)
            batch(0, True, False)
            with pe.Fori(1, B - 1) as b:
                batch(b, False, False)
            batch(B - 1, False, True)
            def turn_norm(k, g):
                pe.wait_ge(s["lat_ready"], 2 + 2 * k + g)
                bank, _ = TURNED[k][g]
                for b in GROUPS[g]:
                    mm = pe.transpose(ps[:, bank, b * 128:b * 128 + 128], xn[:, b, :], ident[:])
                mm.then_inc(s["xT_fill"], 1)

            head_values(B - 1, 1)
            turn_heads(B - 1, 1)
            turn_norm(0, 0)
            project(B - 1)

            pe.wait_ge(s["late_in"], LATE)
            pe.wait_ge(s["const_done"], N_CONST)
            turn_norm(0, 1)
            pe.wait_ge(s["xT_done"], 2)
            for t in range(2):
                pe.matmul(ps[:, 1 + t, :], aw[:, t, :], xT, start=True, stop=True).then_inc(s["a_fill"], 1)
            for b in range(B):
                mm = pe.matmul(ps[:, 3, b * 128:b * 128 + 128], xT[:, b * 128:b * 128 + 128], aw[:, 2, :],
                               start=True, stop=True)
            mm.then_inc(s["a_fill"], 1)
            for g in range(4):
                for t in range(2):
                    pe.wait_ge(s["qk_split"], t + 1)
                    if g >= 2:
                        pe.wait_ge(s["q_stacked" if t == 0 else "k_stacked"], g - 1)
                    for k, part in enumerate((qkh, qkl)):
                        mm = pe.matmul(ps[:, 4 + 2 * (g % 2) + t, :],
                                       pick[:, t, k, g, :, :, :].rearrange("p m r d -> p (m r d)"), part[:, t, :],
                                       start=(k == 0), stop=(k == 1))
                    mm.then_inc(s["qk_fill"], 1)
            STEPS = 4 * B

            def local_scores(k):
                b, g = k // 4, k % 4
                if b == 0:
                    pe.wait_ge(s["q_stacked"], g + 1)
                    pe.wait_ge(s["k_block"], 4 * g + 4)
                if k >= 3:
                    pe.wait_ge(s["a_exp"], k - 2)
                pe.matmul(ps[:, k % 3, :], qks[:, 0, g, b * 128:b * 128 + 128],
                          kblk[:, g, b, :, :].rearrange("p m n -> p (m n)"), start=True, stop=False)
                pe.matmul(ps[:, k % 3, :], identb[:], band[:, None, :].broadcast_to([128, 4, 128]),
                          start=False, stop=True).then_inc(s["a_s"], 1)

            def local_turn(k):
                if k == 0:
                    pe.wait_ge(s["q_stacked"], 4)
                    pe.wait_ge(s["k_stacked"], 4)
                pe.wait_ge(s["a_exp"], k + 1)
                if k >= 2:
                    pe.wait_ge(s["a_trc"], k - 1)
                for m in range(4):
                    mm = pe.transpose(ps[:, 4 + k % 2, m * 128:m * 128 + 128], pa[:, 4 * (k % 4) + m, :], ident[:])
                mm.then_inc(s["a_tr"], 1)

            def local_values(k):
                b, g = k // 4, k % 4
                pe.wait_ge(s["a_trc"], k + 1)
                if k == 0:
                    pe.wait_ge(s["va_done"], 4)
                if b >= 2 and g == 0:
                    pe.wait_ge(s["a_o"], b - 1)
                for m in range(4):
                    c = 9 * (4 * g + m)
                    p, v = [paT[a][:, 4 * (k % 4) + m, :] for a in range(2)], [vap[a][:, b, 4 * g + m, :] for a in range(2)]
                    mm = three(ps[:, 3 + 3 * (b % 2), c:c + 9], p[0], p[1], v[0], v[1])
                mm.then_inc(s["a_pv"], 1)

            local_scores(0)
            local_scores(1)
            for k in range(STEPS + 4):
                if k + 2 < STEPS:
                    local_scores(k + 2)
                if k < STEPS:
                    local_turn(k)
                if 1 <= k <= STEPS:
                    local_values(k - 1)
                if k % 4 == 2 and k >= 6:
                    b = (k - 6) // 4
                    pe.wait_ge(s["a_o"], b + 1)
                    if b >= 1:
                        pe.wait_ge(s["a_x2"], b)
                    pe.transpose(ps[:, 7, 0:128], oa, ident[:]).then_inc(s["a_oT"], 1)
                if k % 4 == 3 and k >= 7:
                    b = (k - 7) // 4
                    pe.wait_ge(s["a_oTc"], b + 1)
                    pe.matmul(ps[:, 7, 0:128], oaT, aw[:, 3, :], start=True, stop=True).then_inc(s["a_y"], 1)

            turn_norm(1, 0)
            turn_norm(1, 1)
            pe.wait_ge(s["xT_done"], 4)
            for b in range(B):
                mm = pe.matmul(ps[:, 7, b * E:b * E + E], xT[:, b * 128:b * 128 + 128], rw_s, start=True, stop=True)
            mm.then_inc(s["r_log"], 1)
            pe.wait_ge(s["xp_done"], 2)

            def expert_out(e):
                pe.wait_ge(s["f_g"], 2 * e + 2)
                if e >= 2:
                    pe.wait_ge(s["f_acc"], B * (e - 1))
                for b in range(B):
                    for k in range(2):
                        mm = pe.matmul(ps[:, 6 + e % 2, b * 128:b * 128 + 128],
                                       gT[0:FH, 2 * e + k, b * 128:b * 128 + 128], w2_s[:, 2 * e + k, :],
                                       start=(k == 0), stop=(k == 1))
                mm.then_inc(s["f_o"], 1)

            for e in range(E):
                pe.wait_ge(s["w_split"], 2 * e + 2)
                for c in (2 * e, 2 * e + 1):
                    if c >= 2:
                        pe.wait_ge(s["f_g"], c - 1)
                    for k in range(2):
                        f = k * F + c % 2 * FH
                        mm = three(ps[0:FH, 2 + 2 * (c % 2) + k, :], w1p[0][:, e, f:f + FH], w1p[1][:, e, f:f + FH],
                                   xTp[0], xTp[1])
                    mm.then_inc(s["f_y"], 1)
                if e >= 1:
                    expert_out(e - 1)
            expert_out(E - 1)

        @block.scalar
        def _(act):
            for k, v in enumerate((g1, b1, g2)):
                act.dma_start(gb[:, k:k + 1], v.rearrange("(p o) -> p o", o=1)).then_inc(s["gb_in"], 16)
            act.sem_inc(s["zT_copied"], 2)
            act.sem_inc(s["rT_copied"], 1)
            act.sem_inc(s["exp_done"], 2)
            act.sem_inc(s["oT_copied"], 1)

            def copy(o, i):
                return act.activation(o, i, ACT.Copy)

            act.wait_ge(s["meta_done"], 1)
            number, before, pairs, pairs_before = counts(act)
            for e in range(N_FILL):
                act.wait_ge(s["fill"], e + 1)
                if e == T_WV:
                    act.wait_ge(s["pool_fold"], 4)
                copy(*prepared(e, 0)).then_inc(s["hi"], 1)
            def turned_pairs(b):
                n, off = pairs(b), pairs_before(b)
                with act.Fori(0, n) as i:
                    u = off + i
                    for c in range(2):
                        act.wait_ge(s["zT_fill"], 2 * u + c + 1)
                        act.sem_inc(s["passed_act"], 1)
                        copy(zcT_pairs[:, bass.ds(u, 1), c, :, :].rearrange("p o a k -> p (o a k)"),
                             ps[:, c, :].bitcast(F16)[:, 0:256]).then_inc(s["zT_copied"], 1)

            def shifts(b):
                act.wait_ge(s["rT_done"], b + 2)
                act.wait_ge(s["row_set"], 64 * b + 64)
                copy(rT, ps[0:64, 3, :].bitcast(F16)[:, 0:128]).then_inc(s["rT_copied"], 1)

            turned_pairs(0)
            act.wait_ge(s["c_done"], 1)
            for i in range(NP):
                copy(mbias.rearrange("p (b i c) -> p b i c", b=B, c=2)[:, :, i, :], mbc[:, :, NP - 1 - i, :]
                     ).then_inc(s["mb_turned"], 1)
            act.wait_ge(s["mb_turned"], NP)
            turned_pairs(1)
            for b in range(1, B - 1):
                shifts(b - 1)
                turned_pairs(b + 1)
            shifts(B - 2)

            def exps(u, bias):
                for k in range(2):
                    act.wait_ge(s["sc_ready"], 2 * u + k + 1)
                    act.wait_ge(s["p_ready"], 2 * u + k + 1)
                    act.sem_inc(s["passed_act"], 1)
                    act.activation(p32[:, k, :], ps[:, k, :], ACT.Exp, bias=bias, scale=XSCALE
                                   ).then_inc(s["exp_done"], 1)

            def sums(t, u):
                act.wait_ge(s["pv_done"], 2 * u + 4)
                act.activation(th[:, t, :], ps[:, 2 + 2 * t:4 + 2 * t, :].rearrange("p k n -> p (k n)"),
                               ACT.Copy, scale=TSCALE).then_inc(s["t_hi"], 1)

            def batch(b, first, last):
                n, off = number(b), before(b)
                for g in range(2):
                    base = 2 * (off + b) + g * (n + 1)
                    exps(base + 1, mbias[:, bass.ds(NC * b, 1)])
                    if first and g == 0:
                        shifts(B - 1)
                    act.wait_ge(s["u_done"], 2 * b + g + 1)
                    sums(1, base)
                    with act.Fori(1, n) as i:
                        exps(base + i + 1, mbias[:, bass.ds(NC * b + i, 1)])
                    if g == 0 or not last:
                        exps(base + n + 1, 0.0)
                    if g == 1 or not first:
                        turned(*((b, 0) if g == 1 else (b - 1, 1)))
                    sums(0, base + n)

            def turned(b, g):
                act.wait_ge(s["oT_fill"], 2 * b + g + 2)
                act.wait_ge(s["xo_done"], b + 1)
                copy(oT[:, 4 * g:4 * g + 4, :].rearrange("p j n -> p (j n)"), ps[:, 6, :]
                     ).then_inc(s["oT_copied"], 1)

            exps(0, 0.0)
            batch(0, True, False)
            with act.Fori(1, B - 1) as b:
                batch(b, False, False)
            batch(B - 1, False, True)
            act.activation(late[:, 12288:16384], zero2[:, 0:1].broadcast_to([128, 4096]), ACT.Copy
                           ).then_inc(s["k_clear"], 1)
            turned(B - 1, 1)

            for k, (bank, columns) in enumerate(TURNED[0]):
                act.wait_ge(s["xT_fill"], 1 + k)
                copy(xT[:, columns], ps[:, bank, columns]).then_inc(s["xT_done"], 1)
            act.wait_ge(s["nb_done"], 1)
            act.wait_ge(s["a_fill"], 1)
            act.activation(qk32[:, 0, :], ps[:, 1, :], ACT.Identity, bias=ab[:, 2:3], scale=-ASCALE
                           ).then_inc(s["qk_32"], 1)
            act.wait_ge(s["a_fill"], 2)
            act.activation(qk32[:, 1, :], ps[:, 2, :], ACT.Identity, bias=ab[:, 1:2]).then_inc(s["qk_32"], 1)
            for g in range(4):
                act.wait_ge(s["qk_fill"], 2 * g + 1)
                copy(qks[:, 0, g, :], ps[:, 4 + 2 * (g % 2), :]).then_inc(s["q_stacked"], 1)
                act.wait_ge(s["qk_fill"], 2 * g + 2)
                copy(qks[:, 1, g, :], ps[:, 5 + 2 * (g % 2), :]).then_inc(s["k_stacked"], 1)
            for k in range(4 * B + 4):
                if k < 4 * B:
                    act.wait_ge(s["a_max"], k + 1)
                    if k >= 4:
                        act.wait_ge(s["a_tr"], k - 3)
                    for m in range(4):
                        h = 4 * (k % 4) + m
                        ins = act.activation(pa[:, h, :], ps[:, k % 3, m * 128:m * 128 + 128], ACT.Exp,
                                             bias=amin[:, k // 4, h:h + 1], scale=-1.0)
                    ins.then_inc(s["a_exp"], 1)
                if 1 <= k <= 4 * B:
                    act.wait_ge(s["a_tr"], k)
                    if k >= 5:
                        act.wait_ge(s["a_pv"], k - 4)
                    c = 4 * ((k - 1) % 4)
                    copy(paT[0][:, c:c + 4, :].rearrange("p h k -> p (h k)"), ps[:, 4 + (k - 1) % 2, :]
                         ).then_inc(s["a_trh"], 1)
                if k % 4 == 2 and k >= 6:
                    b = (k - 6) // 4
                    act.wait_ge(s["a_oT"], b + 1)
                    if b >= 1:
                        act.wait_ge(s["a_y"], b)
                    copy(oaT, ps[:, 7, 0:128]).then_inc(s["a_oTc"], 1)
            for k, (bank, columns) in enumerate(TURNED[1]):
                act.wait_ge(s["xT_fill"], 3 + k)
                copy(xTp[0][:, columns], ps[:, bank, columns])
                copy(xT[:, columns], ps[:, bank, columns]).then_inc(s["xT_done"], 1)
            act.wait_ge(s["r_log"], 2)
            act.activation(ex[:].rearrange("p b e -> p (b e)"), lg[:].rearrange("p b e -> p (b e)"), ACT.Exp
                           ).then_inc(s["r_exp"], 1)
            for c in range(2 * E):
                act.wait_ge(s["f_y"], c + 1)
                if c >= 2:
                    act.wait_ge(s["f_g"], c - 1)
                act.activation(tt[:, c % 2, :], ps[0:FH, 2 + 2 * (c % 2), :], ACT.Tanh, scale=0.5
                               ).then_inc(s["f_t"], 1)

        @block.vector
        def _(dve):
            dve.sem_inc(s["slab_free"], 2)
            dve.sem_inc(s["q_max"], 2)
            dve.sem_inc(s["rT_done"], 1)
            dve.sem_inc(s["p_ready"], 2)
            dve.sem_inc(s["pv_done"], 2)
            dve.sem_inc(s["t_lo"], 2)
            dve.sem_inc(s["u_done"], 1)
            dve.sem_inc(s["x1_done"], 1)
            dve.sem_inc(s["xo_done"], 1)
            dve.sem_inc(s["oT_fill"], 1)
            order = [0]

            def link(ins):
                order[0] += 1
                ins.then_inc(s["seq"], 1)
                dve.wait_ge(s["seq"], order[0])

            def norm(src, k):
                moments(src)
                return rows(src, k)

            def moments(src, batches=range(B)):
                for b in batches:
                    ins = dve.bn_stats(stl[:, b, :], src[:, b, :])
                link(ins)
                for b in batches:
                    ins = dve.bn_aggr(mvl[:, b, :], stl[:, b, :])
                link(ins)
                group = slice(batches[0], batches[-1] + 1)
                dve.tensor_scalar(rsl[:, group], mvl[:, group, 1], EPS, None, ALU.add).then_inc(s["stat_ready"], 1)

            def rows(src, k, batches=range(B)):
                dve.wait_ge(s["rs_ready"], k + 1)
                for b in batches:
                    ins = dve.tensor_scalar(xn[:, b, :], src[:, b, :], mvl[:, b, 0:1], rsl[:, b:b + 1],
                                            ALU.subtract, ALU.mult)
                return ins

            dve.memset(mkb[:], 0.0).then_inc(s["fl_done"], 1)
            dve.memset(st[:], 1.0)
            dve.memset(metaf[:], 0.0)
            for b in range(B):
                dve.memset(place[:, :, b:b + 1], float(64 ** b))
            dve.wait_ge(s["mask_in"], 16)
            dve.tensor_copy(mkf[:], mk[:]).then_inc(s["fl_done"], 1)
            dve.wait_ge(s["fl_done"], 2)
            dve.tensor_reduce(flag[:], mkf[:], AX_X, ALU.max).then_inc(s["fl_done"], 1)
            dve.wait_ge(s["const_done"], 5)
            dve.wait_ge(s["gb_in"], 48)
            dve.wait_ge(s["gb2_in"], 16)
            for t in range(2):
                dve.tensor_scalar(gt[:, t, 0:127], fold[:, 0:127], gb[:, 2 * t:2 * t + 1], None, ALU.mult)
                ins = dve.tensor_copy(gt[:, t, 127:128], gb[:, 2 * t + 1:2 * t + 2])
            ins.then_inc(s["gt_done"], 1)
            dve.wait_ge(s["cnt_done"], 1)
            dve.tensor_scalar(mbc[:].rearrange("p b i c -> p (b i) c"), ps[:, 7, 0:64].rearrange("p (c i) -> p i c", c=2), 1.0, -MASKED, ALU.subtract, ALU.mult).then_inc(s["mb_done"], 1)
            dve.tensor_scalar(mkb[0:B * NP, :], mkf[:], 1.0, -MASKED, ALU.subtract, ALU.mult).then_inc(s["mb_done"], 1)
            link(dve.tensor_tensor(lastc[:], ps[0:1, 6, 0:B * NP], weight[:], ALU.mult))
            link(dve.tensor_reduce(metaf[:, 0:4], lastc[:].rearrange("p (b i) -> p b i", b=B), AX_X, ALU.max))
            link(dve.tensor_scalar(metaf[:, 0:4], metaf[:, 0:4], 2.0, None, ALU.max))
            dve.tensor_copy(metaf[:, 5:6], metaf[:, 0:1])
            dve.tensor_tensor(metaf[:, 6:7], metaf[:, 0:1], metaf[:, 1:2], ALU.add)
            dve.tensor_copy(metaf[:, 8:10], metaf[:, 0:2])
            link(dve.tensor_tensor(metaf[:, 10:12], metaf[:, 0:2], metaf[:, 2:4], ALU.add))
            link(dve.tensor_tensor(metaf[:, 7:8], metaf[:, 10:11], metaf[:, 1:2], ALU.add))
            link(dve.tensor_tensor(place[:], place[:], metaf[:].rearrange("p (k b) -> p k b", b=B), ALU.mult))
            link(dve.tensor_reduce(packf[:], place[:], AX_X, ALU.add))
            dve.tensor_copy(pack[:], packf[:]).then_inc(s["meta_done"], 1)

            dve.wait_ge(s["x_in"], 16)
            moments(xs)
            dve.wait_ge(s["meta_done"], 1)
            number, before, pairs, pairs_before = counts(dve)
            loaded = dve.value_load(pack[0:1, 2:3], min_val=0, max_val=2 ** 24)

            link(rows(xs, 0))
            link(norm(xn, 1))
            link(dve.memset(xn[:, :, 127:128], 1.0))
            xnf = xn[:]
            link(dve.tensor_copy(zl[:, :, 0, :], xnf))
            dve.tensor_tensor(zl[:, :, 1, :], xnf, zl[:, :, 0, :], ALU.subtract).then_inc(s["lat_ready"], 1)

            def low(e):
                dve.wait_ge(s["hi"], e + 1)
                if e == T_LT:
                    dve.wait_ge(s["lo"], e)
                    dve.sem_inc(s["lo"], 1)
                    return
                o, i = prepared(e, 1)
                high = o if T_QT <= e < T_QQ else prepared(e, 0)[0]
                dve.tensor_tensor(o, i, high, ALU.subtract).then_inc(s["lo"], 1)
                if e == T_WQ:
                    dve.wait_ge(s["lo"], e)
                    for k in range(2):
                        dve.tensor_copy(cw[:, :, k, :], wk2[k][:, :, :, 127]).then_inc(s["c_used"], 1)

            def context_moments(b):
                par = b % 2
                n, off = pairs(b), pairs_before(b)
                loads = nc.s_assert_within(dve.snap((loaded >> (b * 6 + 1)) & 31), 1, 2 * NP,
                                           skip_runtime_bounds_check_because="clamped when packed")
                dve.wait_ge(s[f"ctx_in{par}"], 16 * loads)
                dve.sem_inc(s["passed_dve"], 1)
                with dve.Fori(0, n) as i:
                    for c in range(2):
                        ins = dve.bn_stats(st[:].rearrange("p s (i c) k -> p s i c k", c=2)[:, par, bass.ds(i, 1), c, :]
                                           .rearrange("p o k -> p (o k)"),
                                           raw_pairs[:, par, bass.ds(i, 1), c, :].rearrange("p o k -> p (o k)"))
                    ins.then_inc(s["ctx_bn"], 1)

            after = {T_WQ: 0, T_WV + 1: 1, T_QT + 5: 2, T_QQ + 3: 3}
            for e in range(N_FILL):
                low(e)
                if e in after:
                    context_moments(after[e])
            dve.wait_ge(s["c_done"], 1)
            constants = ps[:, 2, 0:4 * B * H].rearrange("p (b h k t) -> p b h k t", b=B, h=H, k=2)
            for t in range(2):
                ins = dve.tensor_copy(c32[:, :, t, :], constants[:, :, :, 0, t])
            link(ins)
            for t in range(2):
                ins = dve.tensor_tensor(c32[:, :, t, :], constants[:, :, :, 1, t], c32[:, :, t, :], ALU.add)
            link(ins)

            def latent_step(b, k):
                base = 4 * pairs_before(b) + 2 * b
                dve.wait_ge(s["q_scores"], base + k + 1)
                dve.tensor_reduce(mt[b % 2][:, 0, 8 * k:8 * k + 8],
                                  ps[:, 4 + 2 * k:6 + 2 * k, :].rearrange("p k (h n) -> p (k h) n", n=128),
                                  AX_X, ALU.max).then_inc(s["q_max"], 1)

            def batch_maxima(b):
                dve.wait_ge(s["q_max"], 4 * (pairs_before(b) + pairs(b)) + 2 * b + 4)
                dve.sem_inc(s["passed_dve"], 1)
                dve.tensor_reduce(mall[:], mt[b % 2].rearrange("p u h -> p h u"), AX_X, ALU.max
                                  ).then_inc(s["r_seq"], 1)

            def batch_shifts(b):
                dve.wait_ge(s["r_seq"], 4 * b + 3)
                dve.tensor_tensor(r32[:], c32[:, b, :, :], mall[:, None, :].broadcast_to([128, 2, H]), ALU.subtract
                                  ).then_inc(s["r_seq"], 1)
                dve.memset(mt[b % 2], 2 * MASKED).then_inc(s["r_seq"], 1)
                dve.wait_ge(s["r_seq"], 4 * b + 5)
                dve.wait_ge(s["rT_done"], b + 1)
                dve.tensor_scalar(rhl[:, 0, :, :], r32[:], SHIFT / XSCALE, None, ALU.add).then_inc(s["r_seq"], 1)
                dve.wait_ge(s["r_seq"], 4 * b + 6)
                dve.scalar_tensor_tensor(out=rhl[:, 1, :, :], in0=r32[:], scalar=SHIFT / XSCALE, in1=rhl[:, 0, :, :],
                                         op0=ALU.add, op1=ALU.subtract).then_inc(s["r_ready"], 1)

            for k in range(2):
                dve.memset(mt[k], 2 * MASKED).then_inc(s["r_seq"], 1)
            dve.wait_ge(s["r_seq"], 2)
            for b in range(B):
                n, off = pairs(b), pairs_before(b)
                latent_step(b, 0)
                if b >= 1:
                    batch_maxima(b - 1)
                latent_step(b, 1)
                if b >= 1:
                    batch_shifts(b - 1)
                with dve.Fori(0, n) as i:
                    for k in range(4):
                        w = 4 + 2 * (k % 2)
                        dve.wait_ge(s["q_scores"], 4 * (off + i) + 2 * b + k + 3)
                        dve.tensor_reduce(mt[b % 2][:, bass.ds(i + 1, 1), 4 * k:4 * k + 4].rearrange("p o h -> p (o h)"),
                                          ps[:, w:w + 2, :].rearrange("p k (h n) -> p (k h) n", n=256),
                                          AX_X, ALU.max).then_inc(s["q_max"], 1)
            batch_maxima(B - 1)
            batch_shifts(B - 1)

            def normalise(b, g):
                q = 2 * b + g
                dve.wait_ge(s["u_done"], q + 2)
                uv = ps[:, 6:8, 0:4 * (DH + 1)].rearrange("p k (h d) -> p k h d", h=4)
                dve.reciprocal(rinv[:].rearrange("p (k h) -> p k h", k=2), uv[:, :, :, DH]).then_inc(s["u_inv"], 1)
                dve.wait_ge(s["u_inv"], q + 1)
                dve.wait_ge(s["oT_fill"], q + 1)
                for k in range(2):
                    ins = dve.tensor_tensor(on[:, 4 * k:4 * k + 4, :], uv[:, k, :, 0:DH],
                                            rinv[:, 4 * k:4 * k + 4, None].broadcast_to([128, 4, DH]), ALU.mult)
                ins.then_inc(s["on_ready"], 1)

            def residual(b):
                dve.wait_ge(s["xo_done"], b + 2)
                row = xs[:, bass.ds(b, 1), :].rearrange("p o d -> p (o d)")
                dve.tensor_tensor(row, ps[:, 7, 0:128], row, ALU.add).then_inc(s["x1_done"], 1)

            def split(u):
                for k in range(2):
                    dve.wait_ge(s["exp_done"], 2 * u + k + 3)
                    dve.wait_ge(s["pv_done"], 2 * u + k + 1)
                    dve.tensor_copy(ph[:, k, :], p32[:, k, :]).then_inc(s["p_hi"], 1)
                    dve.wait_ge(s["p_hi"], 2 * u + k + 1)
                    dve.tensor_tensor(pl[:, k, :], p32[:, k, :], ph[:, k, :], ALU.subtract
                                      ).then_inc(s["p_ready"], 1)

            def sums(b, g, t):
                dve.wait_ge(s["t_hi"], 2 * (2 * b + g) + 2 - t)
                dve.scalar_tensor_tensor(out=tl[:, t, :],
                                         in0=ps[:, 2 + 2 * t:4 + 2 * t, :].rearrange("p k n -> p (k n)"),
                                         scalar=TSCALE, in1=th[:, t, :], op0=ALU.mult, op1=ALU.subtract
                                         ).then_inc(s["t_lo"], 1)

            def batch(b, first, last):
                n, off = number(b), before(b)
                for g in range(2):
                    base = 2 * (off + b) + g * (n + 1)
                    split(base + 1)
                    sums(b, g, 1)
                    if g == 1 or not first:
                        normalise(*((b, 0) if g == 1 else (b - 1, 1)))
                    with dve.Fori(1, n) as i:
                        split(base + i + 1)
                    if g == 0 or not last:
                        split(base + n + 1)
                    sums(b, g, 0)
                    if g == 0 and not first:
                        residual(b - 1)

            split(0)
            batch(0, True, False)
            with dve.Fori(1, B - 1) as b:
                batch(b, False, False)
            batch(B - 1, False, True)
            dve.wait_ge(s["x1_done"], B)
            moments(xs, GROUPS[0])
            normalise(B - 1, 1)
            rows(xs, 2, GROUPS[0]).then_inc(s["lat_ready"], 1)
            residual(B - 1)

            dve.wait_ge(s["x1_done"], B + 1)
            moments(xs, GROUPS[1])
            rows(xs, 3, GROUPS[1]).then_inc(s["lat_ready"], 1)
            dve.wait_ge(s["lat_ready"], 3)
            dve.wait_ge(s["late_in"], LATE)
            dve.wait_ge(s["const_done"], N_CONST)
            dve.tensor_scalar(ab[:, 2:3], ab[:, 0:1], -ASCALE, None, ALU.mult).then_inc(s["nb_done"], 1)
            link(dve.tensor_tensor(xs[:], xs[:], abr[:, 1:2, :].broadcast_to([128, B, D]), ALU.add))
            for t in range(2):
                dve.wait_ge(s["qk_32"], t + 1)
                link(dve.tensor_copy(qkh[:, t, :], qk32[:, t, :]))
                dve.tensor_tensor(qkl[:, t, :], qk32[:, t, :], qkh[:, t, :], ALU.subtract).then_inc(s["qk_split"], 1)
            dve.memset(va[:, :, :, DK:DK + 1], 1.0).then_inc(s["va_done"], 1)
            for g in range(4):
                dve.wait_ge(s["k_stacked"], g + 1)
                dve.wait_ge(s["k_clear"], 1)
                for m in range(4):
                    own = slice(32 * m, 32 * m + 32)
                    dve.tensor_copy(kblk[own, g, :, m, :], qks[own, 1, g, :].rearrange("p (b n) -> p b n", b=B)
                                    ).then_inc(s["k_block"], 1)

            def least(k):
                b, g = k // 4, k % 4
                dve.wait_ge(s["a_s"], k + 1)
                dve.tensor_reduce(amin[:, b, 4 * g:4 * g + 4],
                                  ps[:, k % 3, :].rearrange("p (h k) -> p h k", h=4), AX_X, ALU.min
                                  ).then_inc(s["a_max"], 1)

            least(0)
            for k in range(4 * B + 2):
                if k + 1 < 4 * B:
                    least(k + 1)
                if k == 0:
                    dve.wait_ge(s["a_fill"], 3)
                    dve.tensor_tensor(va[:, :, :, 0:DK], ps[:, 3, :].rearrange("p (b h d) -> p b h d", b=B, h=AH),
                                      abr[:, 0, :].rearrange("p (h d) -> p h d", h=AH)[:, None, :, :]
                                      .broadcast_to([128, B, AH, DK]), ALU.add).then_inc(s["va_done"], 1)
                    dve.wait_ge(s["va_done"], 2)
                    dve.tensor_copy(vap[0], va).then_inc(s["va_done"], 1)
                    dve.wait_ge(s["va_done"], 3)
                    dve.tensor_tensor(vap[1], va, vap[0], ALU.subtract).then_inc(s["va_done"], 1)
                if 1 <= k <= 4 * B:
                    c = 4 * ((k - 1) % 4)
                    high, low_part = [paT[a][:, c:c + 4, :].rearrange("p h k -> p (h k)") for a in range(2)]
                    dve.wait_ge(s["a_trh"], k)
                    dve.tensor_tensor(low_part, ps[:, 4 + (k - 1) % 2, :], high, ALU.subtract).then_inc(s["a_trc"], 1)
                if k % 4 == 1 and k >= 5:
                    b = (k - 5) // 4
                    dve.wait_ge(s["a_pv"], 4 * b + 4)
                    o = ps[:, 3 + 3 * (b % 2), 0:9 * AH].rearrange("p (h d) -> p h d", h=AH)
                    link(dve.reciprocal(ra, o[:, :, DK]))
                    if b >= 1:
                        dve.wait_ge(s["a_oT"], b)
                    dve.tensor_tensor(oa.rearrange("p (h d) -> p h d", h=AH), o[:, :, 0:DK],
                                      ra[:, :, None].broadcast_to([128, AH, DK]), ALU.mult).then_inc(s["a_o"], 1)
                if k % 4 == 0 and k >= 8:
                    b = (k - 8) // 4
                    dve.wait_ge(s["a_y"], b + 1)
                    dve.tensor_tensor(xs[:, b, :], ps[:, 7, 0:128], xs[:, b, :], ALU.add).then_inc(s["a_x2"], 1)
            dve.wait_ge(s["a_x2"], B - 1)
            moments(xs, GROUPS[0])
            dve.wait_ge(s["a_y"], B)
            dve.tensor_tensor(xs[:, B - 1, :], ps[:, 7, 0:128], xs[:, B - 1, :], ALU.add).then_inc(s["a_x2"], 1)

            rows(xs, 4, GROUPS[0]).then_inc(s["lat_ready"], 1)
            dve.wait_ge(s["a_x2"], B)
            moments(xs, GROUPS[1])
            rows(xs, 5, GROUPS[1]).then_inc(s["lat_ready"], 1)
            for k, (bank, columns) in enumerate(TURNED[1]):
                dve.wait_ge(s["xT_done"], 3 + k)
                dve.tensor_tensor(xTp[1][:, columns], ps[:, bank, columns], xTp[0][:, columns], ALU.subtract
                                  ).then_inc(s["xp_done"], 1)
            dve.wait_ge(s["r_log"], 1)
            logits = ps[:, 7, 0:B * E].rearrange("p (b e) -> p b e", b=B)
            link(dve.tensor_reduce(lgm, logits, AX_X, ALU.max))
            dve.tensor_tensor(lg, logits, lgm[:, :, None].broadcast_to([128, B, E]), ALU.subtract
                              ).then_inc(s["r_log"], 1)
            dve.wait_ge(s["r_log"], 2)
            other = lg[:, :, None, :].broadcast_to([128, B, E, E])
            own = lg[:, :, :, None].broadcast_to([128, B, E, E])
            g4 = gtm.rearrange("p (b e) f -> p b e f", b=B)
            e4 = eqm.rearrange("p (b e) f -> p b e f", b=B)
            dve.tensor_tensor(g4, other, own, ALU.is_gt)
            link(dve.tensor_tensor(e4, other, own, ALU.is_equal))
            link(dve.tensor_tensor(e4, e4, tri[:, None, :, :].broadcast_to([128, B, E, E]), ALU.mult))
            link(dve.tensor_tensor(gtm, gtm, eqm, ALU.add))
            dve.tensor_reduce(rank, gtm, AX_X, ALU.add)
            dve.wait_ge(s["r_exp"], 1)
            link(dve.tensor_reduce(sm, ex, AX_X, ALU.add))
            dve.reciprocal(sm, sm)
            link(dve.scalar_tensor_tensor(out=pr[:].rearrange("p b e -> p (b e)"), in0=rank, scalar=1.5,
                                          in1=ex[:].rearrange("p b e -> p (b e)"), op0=ALU.is_lt, op1=ALU.mult))
            link(dve.scalar_tensor_tensor(out=pr, in0=pr, scalar=0.5, in1=sm[:, :, None].broadcast_to([128, B, E]),
                                          op0=ALU.mult, op1=ALU.mult))
            def combine(e):
                dve.wait_ge(s["f_o"], e + 1)
                if e >= 1:
                    dve.wait_ge(s["f_acc"], B * e)
                for b in range(B):
                    dve.scalar_tensor_tensor(out=xs[:, b, :], in0=ps[:, 6 + e % 2, b * 128:b * 128 + 128],
                                             scalar=pr[:, b, e:e + 1], in1=xs[:, b, :],
                                             op0=ALU.mult, op1=ALU.add).then_inc(s["f_acc"], 1)

            for e in range(E):
                for c in (2 * e, 2 * e + 1):
                    bank = 2 + 2 * (c % 2)
                    dve.wait_ge(s["f_t"], c + 1)
                    if c >= 2:
                        dve.wait_ge(s["f_g"], c - 1)
                    link(dve.scalar_tensor_tensor(out=gg[:, c % 2, :], in0=tt[:, c % 2, :], scalar=1.0,
                                                  in1=ps[0:FH, bank, :], op0=ALU.add, op1=ALU.mult))
                    dve.tensor_tensor(gT[0:FH, c, :], gg[:, c % 2, :], ps[0:FH, bank + 1, :], ALU.mult
                                      ).then_inc(s["f_g"], 1)
                if e >= 1:
                    combine(e - 1)
            combine(E - 1)
            dve.wait_ge(s["f_acc"], B * E)
            dve.sem_inc(s["ready_out"], 1)


_INS = ["x", "ctx_1024", "mask_BxS2_bk0", "L0_xattn_g1", "L0_xattn_b1", "L0_xattn_g2", "L0_xattn_b2",
        "L0_xattn_Wq", "L0_xattn_Wkv", "L0_xattn_Wout", "L0_attn_Wq", "L0_attn_bq", "L0_attn_Wk",
        "L0_attn_bk", "L0_attn_Wv", "L0_attn_bv", "L0_attn_Wo", "L0_attn_bo", "L0_ffn_router_weight",
        "L0_ffn_w1", "L0_ffn_w2"]


def kernel(**inputs):
    import numpy as _np
    import concourse.bacc as _bacc
    from concourse import mybir as _mybir
    from concourse.bass_utils import run_bass_kernel_spmd as _run

    nc = _bacc.Bacc("TRN2", target_bir_lowering=False, num_devices=1)
    arrays, args = {}, []
    for name in _INS:
        a = _np.ascontiguousarray(inputs[name])
        arrays[f"in_{name}"] = a
        args.append(nc.dram_tensor(f"in_{name}", a.shape, _mybir.dt.from_np(a.dtype), kind="ExternalInput").ap())
    args.append(nc.dram_tensor("out_x", (4, 128, 128), F32, kind="ExternalOutput").ap())
    perceiver_block(nc, *args)
    r = _run(nc, [arrays], core_ids=[0])
    return r.results[0]["out_x"]
```
